# Optimizing a Trainium2 kernel written in Bass

```python
import numpy as np
import jax
import jax.numpy as jnp

def _softmax(x, axis=-1):
    return jax.nn.softmax(x, axis=axis)

def _gelu(x):
    return jax.nn.gelu(x, approximate=True)

def _silu(x):
    return jax.nn.silu(x)

def _sigmoid(x):
    return jax.nn.sigmoid(x)

def _layernorm(x, axis=-1, eps=1e-05):
    m = jnp.mean(x, axis=axis, keepdims=True)
    v = jnp.var(x, axis=axis, keepdims=True)
    return (x - m) / jnp.sqrt(v + eps)

def _scatter_add(tgt, idx, src, axis=0):
    return tgt.at[idx].add(src)

def _segment_sum(src, seg, n):
    return jax.ops.segment_sum(src, seg, n)
kernel_name = 'mk_lm_tower_d2_tok_ids256_r4_ddc9a3'

def setup_inputs(seed: int=0):
    np.random.seed(seed)
    _w = jnp.asarray

    def _rec_inputs():
        import jax
        import jax.numpy as jnp
        _rk = jax.random.key(seed)
        x = jax.random.randint(jax.random.fold_in(_rk, 1), (32, 512), 0, 128, jnp.int32)
        return x
    x = _rec_inputs()

    def _L0_tok_setup():
        import jax, jax.numpy as jnp
        import numpy as np
        VOCAB = 128
        D = 64
        S = 128
        B = 128
        MAX_LEN = 128
        SEP_ID = 13
        PAD_ID = 1

        def _make_pe():
            pos = np.arange(MAX_LEN, dtype=np.float32)[:, None]
            div = np.exp(np.arange(0, D, 2, dtype=np.float32) * (-np.log(10000.0) / D))
            pe = np.zeros((MAX_LEN, D), dtype=np.float32)
            pe[:, 0::2] = np.sin(pos * div)
            pe[:, 1::2] = np.cos(pos * div)
            return jnp.asarray(pe)
        key = jax.random.key(seed)
        k1, k2 = jax.random.split(key)
        sequence = jax.random.randint(k1, (S, B), 0, VOCAB)
        token_W = jax.random.normal(k2, (VOCAB, D), dtype=jnp.float32) * 0.02
        token_W = token_W.at[0].set(0.0)
        pe = _make_pe()
        return {'sequence': sequence, 'token_W': token_W, 'pe': pe}
    _L0_tok_all = _L0_tok_setup()
    _L0_tok_in = {k: v for k, v in _L0_tok_all.items() if k in ('token_W', 'pe')}
    del _L0_tok_all

    def _L0_attn_setup():
        import jax, jax.numpy as jnp
        import numpy as np
        key = jax.random.key(seed)
        k1, k2, k3 = jax.random.split(key, 3)
        d = 64
        x = jax.random.normal(k1, (8, 512, d), dtype=jnp.float32)
        Wq = jax.random.normal(k2, (d, d), dtype=jnp.float32) * d ** (-0.5)
        Wk = jax.random.normal(k3, (d, d), dtype=jnp.float32) * d ** (-0.5)
        return {'x': x, 'Wq': Wq, 'Wk': Wk}
    _L0_attn_all = _L0_attn_setup()
    _L0_attn_in = {k: v for k, v in _L0_attn_all.items() if k in ('Wq', 'Wk')}
    del _L0_attn_all

    def _L0_ffn_setup():
        import jax, jax.numpy as jnp
        import numpy as np
        B, T, IN_DIM = (64, 64, 64)
        HID, OUT_DIM = (128, 64)
        N_LAYERS, N_EXPERTS, N_SHARED = (2, 16, 1)
        key = jax.random.key(seed)
        ks = jax.random.split(key, 10)
        s = 0.02
        x = jax.random.normal(ks[0], (B, T, IN_DIM), dtype=jnp.float32)
        route_id = jax.random.randint(ks[1], (B,), 0, N_EXPERTS)
        Wi = jax.random.normal(ks[2], (HID, IN_DIM), dtype=jnp.float32) * s
        bi = jnp.zeros((HID,), dtype=jnp.float32)
        Wr = jax.random.normal(ks[3], (N_LAYERS, N_EXPERTS, HID, HID), dtype=jnp.float32) * s
        br = jax.random.normal(ks[4], (N_LAYERS, N_EXPERTS, HID), dtype=jnp.float32) * s
        Ws = jax.random.normal(ks[5], (N_LAYERS, N_SHARED, HID, HID), dtype=jnp.float32) * s
        bs = jax.random.normal(ks[6], (N_LAYERS, N_SHARED, HID), dtype=jnp.float32) * s
        Wo = jax.random.normal(ks[7], (OUT_DIM, HID), dtype=jnp.float32) * s
        bo = jnp.zeros((OUT_DIM,), dtype=jnp.float32)
        return {'x': x, 'route_id': route_id, 'Wi': Wi, 'bi': bi, 'Wr': Wr, 'br': br, 'Ws': Ws, 'bs': bs, 'Wo': Wo, 'bo': bo}
    _L0_ffn_all = _L0_ffn_setup()
    _L0_ffn_in = {k: v for k, v in _L0_ffn_all.items() if k in ('route_id', 'Wi', 'bi', 'Wr', 'br', 'Ws', 'bs', 'Wo', 'bo')}
    del _L0_ffn_all

    def _L1_attn_setup():
        import jax, jax.numpy as jnp
        import numpy as np
        EMBED_DIM = 64
        B, S = (4, 2048)
        key = jax.random.key(seed)
        ks = jax.random.split(key, 9)
        d = EMBED_DIM
        s = 1.0 / np.sqrt(d)
        return {'x': jax.random.normal(ks[0], (B, S, d), dtype=jnp.float32), 'Wq': jax.random.uniform(ks[1], (d, d), jnp.float32, -s, s), 'bq': jax.random.uniform(ks[2], (d,), jnp.float32, -s, s), 'Wk': jax.random.uniform(ks[3], (d, d), jnp.float32, -s, s), 'bk': jax.random.uniform(ks[4], (d,), jnp.float32, -s, s), 'Wv': jax.random.uniform(ks[5], (d, d), jnp.float32, -s, s), 'bv': jax.random.uniform(ks[6], (d,), jnp.float32, -s, s), 'Wo': jax.random.uniform(ks[7], (d, d), jnp.float32, -s, s), 'bo': jax.random.uniform(ks[8], (d,), jnp.float32, -s, s)}
    _L1_attn_all = _L1_attn_setup()
    _L1_attn_in = {k: v for k, v in _L1_attn_all.items() if k in ('Wq', 'bq', 'Wk', 'bk', 'Wv', 'bv', 'Wo', 'bo')}
    del _L1_attn_all

    def _L1_ffn_setup():
        import jax, jax.numpy as jnp
        import numpy as np
        B, S, D, E, H, K = (4, 1024, 64, 8, 128, 2)
        key = jax.random.key(seed)
        ks = jax.random.split(key, 6)
        x = jax.random.normal(ks[0], (B, S, D), jnp.float32)
        Wg = jax.random.normal(ks[1], (D, E), jnp.float32) * 0.02
        bg = jnp.zeros((E,), jnp.float32)
        W1 = jax.random.normal(ks[2], (E, D, H), jnp.float32) * 0.02
        b1 = jnp.zeros((E, H), jnp.float32)
        W2 = jax.random.normal(ks[3], (E, H, D), jnp.float32) * 0.02
        b2 = jnp.zeros((E, D), jnp.float32)
        return {'x': x, 'Wg': Wg, 'bg': bg, 'W1': W1, 'b1': b1, 'W2': W2, 'b2': b2}
    _L1_ffn_all = _L1_ffn_setup()
    _L1_ffn_in = {k: v for k, v in _L1_ffn_all.items() if k in ('Wg', 'bg', 'W1', 'b1', 'W2', 'b2')}
    del _L1_ffn_all
    return {'x': x, 'L0_tok_token_W': _L0_tok_in['token_W'], 'L0_tok_pe': _L0_tok_in['pe'], 'L0_attn_Wq': _L0_attn_in['Wq'], 'L0_attn_Wk': _L0_attn_in['Wk'], 'L0_ffn_route_id': _L0_ffn_in['route_id'], 'L0_ffn_Wi': _L0_ffn_in['Wi'], 'L0_ffn_bi': _L0_ffn_in['bi'], 'L0_ffn_Wr': _L0_ffn_in['Wr'], 'L0_ffn_br': _L0_ffn_in['br'], 'L0_ffn_Ws': _L0_ffn_in['Ws'], 'L0_ffn_bs': _L0_ffn_in['bs'], 'L0_ffn_Wo': _L0_ffn_in['Wo'], 'L0_ffn_bo': _L0_ffn_in['bo'], 'L1_attn_Wq': _L1_attn_in['Wq'], 'L1_attn_bq': _L1_attn_in['bq'], 'L1_attn_Wk': _L1_attn_in['Wk'], 'L1_attn_bk': _L1_attn_in['bk'], 'L1_attn_Wv': _L1_attn_in['Wv'], 'L1_attn_bv': _L1_attn_in['bv'], 'L1_attn_Wo': _L1_attn_in['Wo'], 'L1_attn_bo': _L1_attn_in['bo'], 'L1_ffn_Wg': _L1_ffn_in['Wg'], 'L1_ffn_bg': _L1_ffn_in['bg'], 'L1_ffn_W1': _L1_ffn_in['W1'], 'L1_ffn_b1': _L1_ffn_in['b1'], 'L1_ffn_W2': _L1_ffn_in['W2'], 'L1_ffn_b2': _L1_ffn_in['b2']}

def reference(x, L0_tok_token_W, L0_tok_pe, L0_attn_Wq, L0_attn_Wk, L0_ffn_route_id, L0_ffn_Wi, L0_ffn_bi, L0_ffn_Wr, L0_ffn_br, L0_ffn_Ws, L0_ffn_bs, L0_ffn_Wo, L0_ffn_bo, L1_attn_Wq, L1_attn_bq, L1_attn_Wk, L1_attn_bk, L1_attn_Wv, L1_attn_bv, L1_attn_Wo, L1_attn_bo, L1_ffn_Wg, L1_ffn_bg, L1_ffn_W1, L1_ffn_b1, L1_ffn_W2, L1_ffn_b2):
    import jax
    import jax.numpy as jnp

    def _L0_tok_ref(sequence, token_W, pe):
        import jax, jax.numpy as jnp
        import numpy as np
        VOCAB = 128
        D = 64
        S = 128
        B = 128
        MAX_LEN = 128
        SEP_ID = 13
        PAD_ID = 1

        def _make_pe():
            pos = np.arange(MAX_LEN, dtype=np.float32)[:, None]
            div = np.exp(np.arange(0, D, 2, dtype=np.float32) * (-np.log(10000.0) / D))
            pe = np.zeros((MAX_LEN, D), dtype=np.float32)
            pe[:, 0::2] = np.sin(pos * div)
            pe[:, 1::2] = np.cos(pos * div)
            return jnp.asarray(pe)
        tok_emb = token_W[sequence] * (sequence != 0)[..., None].astype(token_W.dtype)
        S_, B_ = sequence.shape

        def step(carry, xs):
            prev_sep, pad_num = carry
            tok, j = xs
            is_sep = tok == SEP_ID
            skip = prev_sep & (tok == PAD_ID) & ~is_sep
            pos_emb = pe[j - pad_num]
            emb = jnp.where(skip[:, None], jnp.zeros((), pe.dtype), pos_emb)
            new_carry = (is_sep | skip, pad_num + skip.astype(pad_num.dtype))
            return (new_carry, emb)
        init = (jnp.zeros((B_,), dtype=bool), jnp.zeros((B_,), dtype=jnp.int32))
        _, pos_emb = jax.lax.scan(step, init, (sequence, jnp.arange(S_, dtype=jnp.int32)))
        return tok_emb + pos_emb

    def _L0_attn_ref(x, Wq, Wk):
        import jax, jax.numpy as jnp
        import numpy as np
        d = x.shape[-1]
        scale = d ** (-0.5)
        q = jnp.einsum('bnd,ed->bne', x, Wq)
        k = jnp.einsum('bnd,ed->bne', x, Wk)
        sim = jnp.einsum('bid,bjd->bij', q, k) * scale
        attn = jax.nn.softmax(sim, axis=-1)
        out = jnp.einsum('bij,bjd->bid', attn, x)
        return out

    def _L0_ffn_ref(x, route_id, Wi, bi, Wr, br, Ws, bs, Wo, bo):
        import jax, jax.numpy as jnp
        import numpy as np
        B, T, IN_DIM = (64, 64, 64)
        HID, OUT_DIM = (128, 64)
        N_LAYERS, N_EXPERTS, N_SHARED = (2, 16, 1)
        flat = x.reshape(-1, x.shape[-1])
        n_tok = flat.shape[0]
        route = jnp.repeat(route_id, n_tok // route_id.shape[0])
        h = jax.nn.relu(flat @ Wi.T + bi)
        n_layers, n_experts = (Wr.shape[0], Wr.shape[1])
        for l in range(n_layers):
            shared = (jnp.einsum('nd,shd->snh', h, Ws[l]) + bs[l][:, None, :]).mean(axis=0)
            routed = jnp.zeros_like(h)
            for e in range(n_experts):
                ye = h @ Wr[l, e].T + br[l, e]
                routed = routed + jnp.where((route == e)[:, None], ye, 0.0)
            h = jax.nn.relu(shared + routed + h)
        out = h @ Wo.T + bo
        return out.reshape(*x.shape[:-1], out.shape[-1])

    def _L1_attn_ref(x, Wq, bq, Wk, bk, Wv, bv, Wo, bo):
        import jax, jax.numpy as jnp
        import numpy as np
        EMBED_DIM = 64
        B, S = (4, 2048)
        d = x.shape[-1]
        scaling = d ** (-0.5)
        q = x @ Wq.T + bq
        k = x @ Wk.T + bk
        v = x @ Wv.T + bv
        scores = jnp.einsum('bsd,btd->bst', q, k) * scaling
        weights = jax.nn.softmax(scores, axis=-1)
        attn = jnp.einsum('bst,btd->bsd', weights, v)
        return attn @ Wo.T + bo

    def _L1_ffn_ref(x, Wg, bg, W1, b1, W2, b2):
        import jax, jax.numpy as jnp
        import numpy as np
        B, S, D, E, H, K = (4, 1024, 64, 8, 128, 2)
        Bv, Sv, Dv = x.shape
        gate_scores = x @ Wg + bg
        _, idx = jax.lax.top_k(gate_scores, K)
        mask = jax.nn.one_hot(idx, E, dtype=x.dtype).sum(axis=-2)
        xf = x.reshape(-1, Dv)
        mf = mask.reshape(-1, E)
        h = jax.nn.gelu(jnp.einsum('td,edh->teh', xf, W1) + b1[None], approximate=False)
        y = jnp.einsum('teh,ehd->ted', h, W2) + b2[None]
        out = jnp.einsum('ted,te->td', y, mf)
        return out.reshape(Bv, Sv, Dv)
    h = _L0_tok_ref(x, L0_tok_token_W, L0_tok_pe)
    h = h + _L0_attn_ref(_layernorm(h, axis=-1), L0_attn_Wq, L0_attn_Wk)
    h = h + _L0_ffn_ref(_layernorm(h, axis=-1), L0_ffn_route_id, L0_ffn_Wi, L0_ffn_bi, L0_ffn_Wr, L0_ffn_br, L0_ffn_Ws, L0_ffn_bs, L0_ffn_Wo, L0_ffn_bo)
    h = h + _L1_attn_ref(_layernorm(h, axis=-1), L1_attn_Wq, L1_attn_bq, L1_attn_Wk, L1_attn_bk, L1_attn_Wv, L1_attn_bv, L1_attn_Wo, L1_attn_bo)
    h = h + _L1_ffn_ref(_layernorm(h, axis=-1), L1_ffn_Wg, L1_ffn_bg, L1_ffn_W1, L1_ffn_b1, L1_ffn_W2, L1_ffn_b2)
    return h

_drawn_inputs = setup_inputs


def setup_inputs(seed=0):
    import zlib

    import numpy as np

    out = dict(_drawn_inputs(seed))
    spreads = {'L0_ffn_bi': (0.0, 0.463),
     'L0_ffn_bo': (0.0, 0.1),
     'L1_ffn_bg': (0.0, 0.1),
     'L1_ffn_b1': (0.0, 0.759),
     'L1_ffn_b2': (0.0, 0.1)}
    factors = {'L0_tok_token_W': 3.15,
     'L0_attn_Wq': 8.0,
     'L0_attn_Wk': 8.0,
     'L0_ffn_Wr': 6.517,
     'L0_ffn_br': 6.755,
     'L0_ffn_Ws': 5.324,
     'L0_ffn_bs': 6.359,
     'L1_attn_Wq': 8.0,
     'L1_attn_bq': 46.246,
     'L1_attn_Wk': 8.0,
     'L1_attn_bk': 64.0,
     'L1_ffn_W1': 3.301,
     'L1_ffn_W2': 2.739}
    for name, (base, spread) in spreads.items():
        noise = np.random.default_rng([zlib.crc32(name.encode()), seed]).standard_normal(out[name].shape)
        drawn = base * np.exp(spread * noise) if base else spread * noise
        out[name] = jnp.asarray(drawn.astype(out[name].dtype))
    for name, factor in factors.items():
        out[name] = (out[name] * factor).astype(out[name].dtype)
    return out
```

```python
from contextlib import ExitStack

import numpy as np

import concourse.bass as bass
from concourse import mybir

F32 = mybir.dt.float32
F32R = mybir.dt.float32r
I32 = mybir.dt.int32
ALU = mybir.AluOpType
ACT = mybir.ActivationFunctionType
AX = mybir.AxisListType.X

P = 128
NSEQ, SEQ, D = 32, 512, 64
NT = SEQ // P
HID = 128
NEXP0, NLAY0 = 16, 2
NEXP1, TOPK = 8, 2
VOCAB = 128
SEP_ID, PAD_ID = 13, 1
EPS = 1e-5
CONSTS = 5
SCALE = D ** -0.5
GROUP = SEQ * NSEQ // 64
NG = SEQ // GROUP
WROW = HID + 1
OFF = -(2.0 ** 100)

SPLIT = [("wq1", P), ("wk1", P), ("wi", HID), ("w1", NEXP1 * HID), ("wg", NEXP1),
         ("tok", D), ("pe", D), ("b2", D)]
PLAIN = [("sel", NEXP1 * HID), ("wq0", P), ("wk0", P), ("wv", P), ("wo1", D), ("bvc", P),
         ("wo0", D), ("w2", NEXP1 * D), ("b1", NEXP1), ("bi", 1), ("bq", 1), ("bk", 1),
         ("bo0", D), ("bg", NEXP1), ("ident", P), ("iota", 1), ("steps", NSEQ * NT),
         ("before", NEXP1 * NEXP1), ("after", NEXP1 * NEXP1), ("ws", NLAY0 * WROW)]


def columns():
    at, n = {}, 0
    for name, width in SPLIT + PLAIN:
        at[name] = (n, n + width)
        n += width
    return at, n


class NormSignals:

    def __init__(self, sem, tag):
        self.xh_done = sem(f"{tag}_xh_done")
        self.sqsum_ready = sem(f"{tag}_sqsum_ready")
        self.sum_ready = sem(f"{tag}_sum_ready")
        self.sq_ready = sem(f"{tag}_sq_ready")
        self.var_ready = sem(f"{tag}_var_ready")
        self.xs_ready = sem(f"{tag}_xs_ready")
        self.xt_ready = sem(f"{tag}_xt_ready")
        self.x2_ready = sem(f"{tag}_x2_ready")
        self.h_done = sem(f"{tag}_h_done")


class AttentionSignals(NormSignals):

    def __init__(self, sem, tag):
        super().__init__(sem, tag)
        self.k2_ready = sem(f"{tag}_k2_ready")
        self.v_ready = sem(f"{tag}_v_ready")
        self.q_ps = sem(f"{tag}_q_ps")
        self.qh_ready = sem(f"{tag}_qh_ready")
        self.ql_ready = sem(f"{tag}_ql_ready")
        self.s_ps = sem(f"{tag}_s_ps")
        self.max_ready = sem(f"{tag}_max_ready")
        self.m_ps = sem(f"{tag}_m_ps")
        self.m_ready = sem(f"{tag}_m_ready")
        self.st_ps = sem(f"{tag}_st_ps")
        self.e_ready = sem(f"{tag}_e_ready")
        self.o_ps = sem(f"{tag}_o_ps")
        self.k_ps = sem(f"{tag}_k_ps")
        self.kh_ready = sem(f"{tag}_kh_ready")
        self.kl_ready = sem(f"{tag}_kl_ready")
        self.v_ps = sem(f"{tag}_v_ps")


class RoutedSignals(NormSignals):

    def __init__(self, sem, tag):
        super().__init__(sem, tag)
        self.wc_ready = sem(f"{tag}_wc_ready")
        self.wi_ps = sem(f"{tag}_wi_ps")
        self.h0_ready = sem(f"{tag}_h0_ready")
        self.l0_ps = sem(f"{tag}_l0_ps")
        self.h1_ready = sem(f"{tag}_h1_ready")
        self.l1_ps = sem(f"{tag}_l1_ps")
        self.h2_ready = sem(f"{tag}_h2_ready")
        self.o_ps = sem(f"{tag}_o_ps")


class MixtureSignals(NormSignals):

    def __init__(self, sem, tag):
        super().__init__(sem, tag)
        self.xh_ready = sem(f"{tag}_xh_ready")
        self.g_ps = sem(f"{tag}_g_ps")
        self.mk_ready = sem(f"{tag}_mk_ready")
        self.b2_ps = sem(f"{tag}_b2_ps")
        self.mt_ps = sem(f"{tag}_mt_ps")
        self.m2_ready = sem(f"{tag}_m2_ready")
        self.u_ps = sem(f"{tag}_u_ps")
        self.gelu_ready = sem(f"{tag}_gelu_ready")
        self.o_ps = sem(f"{tag}_o_ps")


def sweep(eng, body, first=2, last=NSEQ - 4):
    for i in range(first):
        body(i, i % 2)
    with eng.Fori(first // 2, last // 2) as pair:
        body(pair * 2, 0)
        body(pair * 2 + 1, 1)
    for i in range(last, NSEQ):
        body(i, i % 2)


def known(i):
    return isinstance(i, int)


def has(i):
    return not known(i) or i < NSEQ


def tower_kernel(nc, tokens, route, pack, experts, out, pos_dram):
    at, width = columns()
    n_split = at[SPLIT[-1][0]][1]

    with ExitStack() as ctx:
        def sb(name, shape, dt=F32):
            return ctx.enter_context(nc.sbuf_tensor(name, shape, dt))

        def ps(name):
            return ctx.enter_context(nc.psum_tensor(name, [P, 512], F32))

        def sem(name):
            return ctx.enter_context(nc.semaphore(name))

        H = sb("H", [P, NSEQ, NT, D])
        W = sb("W", [P, width])
        WH = sb("WH", [P, n_split], F32R)
        WL = sb("WL", [P, n_split], F32R)
        WX = sb("WX", [P, NEXP0, NLAY0 * WROW])
        WS = sb("WS", [P, NLAY0 * WROW])
        WC = sb("WC", [P, 2, NG, NLAY0 * WROW])
        AH = sb("AH", [P, P], F32R)
        AL = sb("AL", [P, P], F32R)
        VH = sb("VH", [P, D], F32R)
        VL = sb("VL", [P, D], F32R)
        VB = sb("VB", [P, D])
        IR = sb("IR", [P, P], F32R)
        half = sb("half", [P, NT])
        ninv = sb("ninv", [P, NT])
        route_sb = sb("route_sb", [1, NSEQ * NG], I32)

        tk = sb("tk", [P, NSEQ * NT], I32)
        sc = [sb(f"sc{k}", [P, NSEQ * NT]) for k in range(8)]
        idb = sb("idb", [P, 2, SEQ], I32)
        posb = sb("posb", [NSEQ, 2, SEQ])
        OH = sb("OH", [P, 2, SEQ], F32R)
        OP = sb("OP", [NSEQ, 2, SEQ], F32R)

        stat = sb("stat", [P, 2, 4, NT])
        var = sb("var", [P, NT])
        XC = sb("XC", [P, NT, D])
        SQ = sb("SQ", [P, NT, D])
        XN = sb("XN", [P, 2, NT, D])
        XS = sb("XS", [P, 2, NT, 2 * D], F32R)
        X2 = sb("X2", [P, 2, SEQ], F32R)
        KS = sb("KS", [P, 2, SEQ], F32R)
        K2 = sb("K2", [P, 2, SEQ], F32R)
        QH = sb("QH", [P, 2, SEQ], F32R)
        Q2 = sb("Q2", [P, 2, SEQ], F32R)
        V1 = sb("V1", [P, 2, NT, D + 1])
        PT = sb("PT", [P, 2, NT, SEQ])
        nmax = sb("nmax", [P, 2, NT], F32R)
        rec = sb("rec", [P, NT])
        ON = sb("ON", [P, NT, D])
        F0 = sb("F0", [P, 2, SEQ])
        F1 = sb("F1", [P, 2, SEQ])
        F2 = sb("F2", [P, 2, SEQ])
        G = sb("G", [P, 2, NEXP1, SEQ])
        gs = sb("gs", [P, NT, NEXP1])
        cge = sb("cge", [P, NT, NEXP1, NEXP1])
        cgt = sb("cgt", [P, NT, NEXP1, NEXP1])
        rank = sb("rank", [P, NT, NEXP1])
        MK = sb("MK", [P, NT, P])

        bank = [ps(f"bank{k}") for k in range(8)]

        def w(name, rows=P):
            a, b = at[name]
            return W[0:rows, a:b]

        def wh(name, rows=P):
            a, b = at[name]
            return WH[0:rows, a:b]

        def wl(name, rows=P):
            a, b = at[name]
            return WL[0:rows, a:b]

        def f32(ap):
            return ap.bitcast(F32)

        def hb(i):
            return H[:, bass.ds(i, 1), :, :].rearrange("p a t d -> p (a t) d")

        def over(ap, n):
            return ap.unsqueeze(2).to_broadcast([P, NT, n])

        tok_in, pack_in, experts_in, route_in = sem("tok_in"), sem("pack_in"), sem("experts_in"), sem("route_in")
        pos_out, ids_in, pos_in, stored = sem("pos_out"), [sem("ids_in0"), sem("ids_in1")], [sem("pos_in0"), sem("pos_in1")], sem("stored")
        dve_chain, pool_chain = sem("dve_chain"), sem("pool_chain")
        consts_set, parts_ready, prod_ready, prod_read = (
            sem("consts_set"), sem("parts_ready"), sem("prod_ready"), sem("prod_read"))
        oh_ready, op_ready, emb_ready, h0_ready = sem("oh_ready"), sem("op_ready"), sem("emb_ready"), sem("h0_ready")

        a0, a1 = AttentionSignals(sem, "a0"), AttentionSignals(sem, "a1")
        f0, f1 = RoutedSignals(sem, "f0"), MixtureSignals(sem, "f1")

        block = ctx.enter_context(nc.Block())

        @block.sync
        def _(sp):
            sp.dma_start(tk[:, :].rearrange("p (s t) -> p s t", t=NT),
                         tokens.rearrange("s (p t) -> p s t", t=NT)).then_inc(tok_in, 16)
            sp.dma_start(W[:, :], pack).then_inc(pack_in, 16)
            sp.dma_start(route_sb[:, :], route).then_inc(route_in, 16)
            sp.dma_start(WX[:, :, :], experts).then_inc(experts_in, 16)
            sp.wait_ge(parts_ready, 1)
            sp.dma_start(pos_dram.rearrange("s (p t) -> p s t", t=NT),
                         sc[7][:, :].rearrange("p (s t) -> p s t", t=NT)).then_inc(pos_out, 16)
            sp.wait_ge(pos_out, 16)

            def load_ids(i, par):
                if not known(i) or i >= 2:
                    sp.wait_ge(oh_ready, i - 1)
                    sp.wait_ge(op_ready, i - 1)
                sp.dma_start(idb[:, par, :], tokens[bass.ds(i, 1), :].to_broadcast([P, SEQ])).then_inc(ids_in[par], 16)
                sp.dma_start(posb[:, par, :],
                             pos_dram[bass.ds(i, 1), :].to_broadcast([NSEQ, SEQ])).then_inc(pos_in[par], 16)

            sweep(sp, load_ids)
            out_rows = out.rearrange("b (p t) d -> p b (t d)", t=NT)

            def store(i, par):
                sp.wait_ge(f1.h_done, i + 1)
                sp.dma_start(out_rows[:, bass.ds(i, 1), :],
                             H[:, bass.ds(i, 1), :, :].rearrange("p a t d -> p a (t d)")).then_inc(stored, 16)

            sweep(sp, store)
            sp.wait_ge(stored, 16 * NSEQ)

        @block.gpsimd
        def _(pool):
            pl = nc.gpsimd

            def then(ins):
                ins.then_inc(pool_chain, 1)

            pl.memset(half[:, :], -0.5).then_inc(consts_set, 1)
            pl.memset(ninv[:, :], -1.0 / D).then_inc(consts_set, 1)
            pl.memset(V1[:, :, :, :], 1.0).then_inc(consts_set, 1)
            pl.memset(f32(K2[:, :, :]), 1.0).then_inc(consts_set, 1)
            pl.memset(MK[:, :, :], 0.0).then_inc(consts_set, 1)

            pool.wait_ge(consts_set, CONSTS)

            STEPS = 4

            def norm_centre(s, base, i, par):
                pool.wait_ge(s.sum_ready, i + 1)
                c = base + i * STEPS
                then(pl.tensor_tensor(stat[:, par, 1, :], stat[:, par, 0, :], ninv[:, :], ALU.mult))
                pool.wait_ge(pool_chain, c + 1)
                then(pl.tensor_tensor(XC[:, :, :], hb(i), over(stat[:, par, 1, :], D), ALU.add))
                pool.wait_ge(pool_chain, c + 2)
                pl.tensor_tensor(SQ[:, :, :], XC[:, :, :], XC[:, :, :], ALU.mult).then_inc(s.sq_ready, 1)

            def norm_scale(s, base, i, par):
                c = base + i * STEPS + 2
                pool.wait_ge(s.var_ready, i + 1)
                then(pl.tensor_tensor(stat[:, par, 3, :], stat[:, par, 2, :], half[:, :], ALU.pow))
                pool.wait_ge(pool_chain, c + 1)
                scale = over(stat[:, par, 3, :], D)
                then(pl.tensor_tensor(XN[:, par, :, :], XC[:, :, :], scale, ALU.mult))
                if not known(i) or i >= 2:
                    pool.wait_ge(s.xt_ready, i - 1)
                pl.tensor_tensor(XS[:, par, :, 0:D], XC[:, :, :], scale, ALU.mult).then_inc(s.xh_done, 1)
                pool.wait_ge(pool_chain, c + 2)
                pool.wait_ge(s.xh_done, i + 1)
                pl.tensor_tensor(XS[:, par, :, D:2 * D], XN[:, par, :, :], f32(XS[:, par, :, 0:D]),
                                 ALU.subtract).then_inc(s.xs_ready, 1)

            def norm(s, base, i, par):
                norm_centre(s, base, i, par)
                norm_scale(s, base, i, par)

            def norms(s, base):
                for i in range(3):
                    norm(s, base, i, i % 2)

                def body(i, par):
                    if has(i + 3):
                        norm(s, base, i + 3, 1 - par)

                sweep(pool, body)

            pool.wait_ge(h0_ready, NSEQ)
            norms(a0, 0)
            pool.wait_ge(a0.h_done, NSEQ)
            norms(f0, NSEQ * STEPS)
            pool.wait_ge(f0.h_done, NSEQ)
            norms(a1, 2 * NSEQ * STEPS)
            pool.wait_ge(a1.h_done, NSEQ)
            norms(f1, 3 * NSEQ * STEPS)

        @block.scalar
        def _(act):
            sc_ = nc.scalar

            def embed(i, par):
                act.wait_ge(emb_ready, i + 1)
                sc_.activation(hb(i), bank[par][:, 0:NT * D].rearrange("p (t d) -> p t d", t=NT),
                               ACT.Copy).then_inc(h0_ready, 1)

            sweep(act, embed)

            def evac_x(s, i, par):
                act.wait_ge(s.xt_ready, i + 1)
                sc_.activation(X2[:, par, :], bank[0][:, :], ACT.Copy).then_inc(s.x2_ready, 1)

            def attention(s, layer):
                def evac_q(i, par):
                    act.wait_ge(s.q_ps, i + 1)
                    if layer == 0:
                        sc_.activation(QH[:, par, :], bank[1][:, :], ACT.Copy).then_inc(s.qh_ready, 1)
                    else:
                        sc_.activation(QH[:, par, :], bank[1][:, :], ACT.Identity,
                                       bias=w("bq")).then_inc(s.qh_ready, 1)
                        act.wait_ge(s.k_ps, i + 1)
                        sc_.activation(KS[:, par, :], bank[0][:, :], ACT.Identity,
                                       bias=w("bk")).then_inc(s.kh_ready, 1)

                evac_x(s, 0, 0)
                evac_q(0, 0)
                evac_x(s, 1, 1)

                def body(i, par):
                    act.wait_ge(s.m_ps, i + 1)
                    sc_.activation(Q2[D:D + 1, par, :], bank[7][D:D + 1, :], ACT.Copy).then_inc(s.m_ready, 1)
                    if has(i + 1):
                        evac_q(i + 1, 1 - par)
                    for kt in range(NT):
                        act.wait_ge(s.st_ps, i * NT + (kt + 1))
                        if kt == 0 and (not known(i) or i >= 2):
                            act.wait_ge(s.o_ps, i - 1)
                        sc_.activation(PT[:, par, kt, :], bank[4 + kt % 2][:, :], ACT.Exp,
                                       scale=SCALE).then_inc(s.e_ready, 1)
                    if has(i + 2):
                        evac_x(s, i + 2, par)

                sweep(act, body)

            act.wait_ge(pack_in, 16)
            attention(a0, 0)
            act.wait_ge(a0.h_done, NSEQ)

            def ffn0_in(i, par):
                act.wait_ge(f0.wi_ps, i + 1)
                sc_.activation(F0[:, par, :], bank[1][:, :], ACT.Relu, bias=w("bi")).then_inc(f0.h0_ready, 1)

            evac_x(f0, 0, 0)
            ffn0_in(0, 0)
            evac_x(f0, 1, 1)

            def ffn0(i, par):
                if has(i + 2):
                    evac_x(f0, i + 2, par)
                if has(i + 1):
                    ffn0_in(i + 1, 1 - par)
                act.wait_ge(f0.l0_ps, i + 1)
                act.wait_ge(f0.wc_ready, i + 1)
                for g in range(NG):
                    ins = sc_.activation(group(F1[:, par, :], g), group(bank[2][:, :], g), ACT.Relu,
                                         bias=WC[:, par, g, HID:HID + 1])
                ins.then_inc(f0.h1_ready, 1)

            def group(ap, g):
                return ap.rearrange("k (t g p) -> k g t p", t=NT, g=NG)[:, g, :, :]

            sweep(act, ffn0)
            act.wait_ge(f0.h_done, NSEQ)
            attention(a1, 1)
            act.wait_ge(a1.h_done, NSEQ)

            def masks(i, par):
                act.wait_ge(f1.mt_ps, i + 1)
                if not known(i) or i >= 2:
                    act.wait_ge(f1.b2_ps, i - 1)
                sc_.activation(K2[D:D + 2 * NEXP1, par, :], bank[2][D:D + 2 * NEXP1, :],
                               ACT.Copy).then_inc(f1.m2_ready, 1)

            evac_x(f1, 0, 0)
            evac_x(f1, 1, 1)
            masks(0, 0)

            def ffn1(i, par):
                for e in range(NEXP1):
                    act.wait_ge(f1.u_ps, i * NEXP1 + (e + 1))
                    if e == 0 and (not known(i) or i >= 2):
                        act.wait_ge(f1.o_ps, i - 1)
                    sc_.activation(G[:, par, e, :], bank[3 + e % 3][:, :], ACT.Gelu,
                                   bias=W[:, at["b1"][0] + e:at["b1"][0] + e + 1]).then_inc(f1.gelu_ready, 1)
                if has(i + 1):
                    masks(i + 1, 1 - par)
                if has(i + 2):
                    evac_x(f1, i + 2, par)

            sweep(act, ffn1)

        @block.vector
        def _(dve):
            v = nc.vector
            count = [0]

            def link(ins):
                count[0] += 1
                ins.then_inc(dve_chain, 1)
                dve.wait_ge(dve_chain, count[0])

            dve.wait_ge(tok_in, 16)
            sep, pad, run, all_pad, t0, t1, skip, pos = (x[:, :] for x in sc)
            link(v.tensor_scalar(sep, tk[:, :], float(SEP_ID), None, ALU.is_equal))
            link(v.tensor_scalar(pad, tk[:, :], float(PAD_ID), None, ALU.is_equal))
            link(v.tensor_copy(all_pad, pad))
            dist = 1
            while dist < NSEQ:
                k = dist * NT
                link(v.tensor_tensor(t0[:, k:], all_pad[:, k:], sep[:, :-k], ALU.mult))
                link(v.tensor_tensor(t1[:, k:], all_pad[:, k:], all_pad[:, :-k], ALU.mult))
                link(v.tensor_tensor(sep[:, k:], sep[:, k:], t0[:, k:], ALU.max))
                link(v.tensor_copy(all_pad[:, k:], t1[:, k:]))
                dist *= 2
            link(v.memset(skip[:, 0:NT], 0.0))
            link(v.tensor_tensor(skip[:, NT:], pad[:, NT:], sep[:, :-NT], ALU.mult))
            link(v.memset(run[:, 0:NT], 0.0))
            link(v.tensor_copy(run[:, NT:], skip[:, :-NT]))
            dist = 1
            while dist < NSEQ:
                k = dist * NT
                link(v.tensor_tensor(t0[:, k:], run[:, k:], run[:, :-k], ALU.add))
                link(v.tensor_copy(run[:, k:], t0[:, k:]))
                dist *= 2
            dve.wait_ge(pack_in, 16)
            link(v.tensor_tensor(pos, w("steps"), run, ALU.subtract))
            link(v.scalar_tensor_tensor(pos, skip, -2.0 * NSEQ, pos, ALU.mult, ALU.add))
            v.tensor_copy(sc[7][:, :], pos).then_inc(parts_ready, 1)

            link(v.memset(w("tok", 1), 0.0))
            link(v.tensor_copy(WH[:, :], W[:, 0:n_split]))
            link(v.tensor_tensor(WL[:, :], W[:, 0:n_split], f32(WH[:, :]), ALU.subtract))
            link(v.tensor_copy(WL[D:P, at["w1"][0]:at["w1"][1]], W[D:P, at["sel"][0]:at["sel"][1]]))
            link(v.tensor_copy(IR[:, :], w("ident")))
            v.tensor_copy(WS[:, :], w("ws")).then_inc(parts_ready, 1)
            dve.wait_ge(parts_ready, 2)
            for l in range(NLAY0):
                link(v.tensor_tensor(WS[:, l * WROW:l * WROW + HID], WS[:, l * WROW:l * WROW + HID],
                                     w("ident"), ALU.add))
            dve.wait_ge(prod_ready, 1)
            link(v.tensor_copy(AH[:, :], bank[5][:, 0:P]))
            link(v.tensor_tensor(AL[:, :], bank[5][:, 0:P], f32(AH[:, :]), ALU.subtract))
            link(v.tensor_copy(VH[:, :], bank[6][:, 0:D]))
            link(v.tensor_tensor(VL[:, :], bank[6][:, 0:D], f32(VH[:, :]), ALU.subtract))
            v.tensor_copy(VB[:, :], bank[7][:, 0:D]).then_inc(prod_read, 1)

            def one_hots(i, par):
                dve.wait_ge(ids_in[par], i * 8 + (16 - 8 * par))
                if not known(i) or i >= 2:
                    dve.wait_ge(emb_ready, i - 1)
                v.tensor_scalar(OH[:, par, :].rearrange("k (t p) -> k t p", t=NT),
                                idb[:, par, :].rearrange("k (p t) -> k t p", t=NT),
                                w("iota"), None, ALU.is_equal).then_inc(oh_ready, 1)
                dve.wait_ge(pos_in[par], i * 8 + (16 - 8 * par))
                v.tensor_scalar(OP[:, par, :].rearrange("k (t p) -> k t p", t=NT),
                                posb[:, par, :].rearrange("k (p t) -> k t p", t=NT),
                                w("iota", NSEQ), None, ALU.is_equal).then_inc(op_ready, 1)

            sweep(dve, one_hots)

            def norm_sum(s, i, par):
                v.tensor_reduce(stat[:, par, 0, :], hb(i), axis=AX, op=ALU.add).then_inc(s.sum_ready, 1)

            def norm_squares(s, i, par):
                dve.wait_ge(s.sq_ready, i + 1)
                v.tensor_reduce(var[:, :], SQ[:, :, :], axis=AX, op=ALU.add).then_inc(s.sqsum_ready, 1)
                dve.wait_ge(s.sqsum_ready, i + 1)
                v.tensor_scalar(stat[:, par, 2, :], var[:, :], 1.0 / D, EPS, ALU.mult, ALU.add)\
                    .then_inc(s.var_ready, 1)

            def copy_v(s, i, par):
                if not known(i) or i >= 2:
                    dve.wait_ge(s.o_ps, i - 1)
                dve.wait_ge(s.xs_ready, i + 1)
                dve.wait_ge(consts_set, CONSTS)
                v.tensor_copy(V1[:, par, :, 0:D], XN[:, par, :, :]).then_inc(s.v_ready, 1)

            def copy_k(s, keys, made, i, par):
                dve.wait_ge(made, i + 1)
                if not known(i) or i >= 2:
                    dve.wait_ge(s.st_ps, i * 4 - 4)
                dve.wait_ge(consts_set, CONSTS)
                v.tensor_copy(K2[0:D, par, :], f32(keys[0:D, par, :])).then_inc(s.k2_ready, 1)

            def attention(s, base, layer):
                keys, made = (X2, s.x2_ready) if layer == 0 else (KS, s.kh_ready)

                def low_parts(i, par):
                    dve.wait_ge(s.qh_ready, i + 1)
                    if layer == 0:
                        v.tensor_tensor(Q2[0:D, par, :], bank[1][0:D, :], f32(QH[0:D, par, :]),
                                        ALU.subtract).then_inc(s.ql_ready, 1)
                        return
                    v.scalar_tensor_tensor(Q2[0:D, par, :], bank[1][0:D, :], w("bq", D), f32(QH[0:D, par, :]),
                                           ALU.add, ALU.subtract).then_inc(s.ql_ready, 1)
                    dve.wait_ge(s.kh_ready, i + 1)
                    a = at["bk"][0]
                    v.scalar_tensor_tensor(KS[D:P, par, :], bank[0][D:P, :], W[D:P, a:a + 1],
                                           f32(KS[D:P, par, :]), ALU.add, ALU.subtract).then_inc(s.kl_ready, 1)
                    dve.wait_ge(s.v_ps, i + 1)
                    v.tensor_tensor(V1[:, par, :, 0:D], bank[2][:, 0:NT * D].rearrange("p (t d) -> p t d", t=NT),
                                    VB[:, :].unsqueeze(1).to_broadcast([P, NT, D]), ALU.add).then_inc(s.v_ready, 1)

                def maxima(i, par):
                    for t in range(NT):
                        dve.wait_ge(s.s_ps, i * NT + (t + 1))
                        v.tensor_reduce(nmax[:, par, t:t + 1], bank[2 + t % 2][:, :], axis=AX, op=ALU.max,
                                        negate=True).then_inc(s.max_ready, 1)

                def finish(i, par):
                    o = bank[6][:, 0:NT * (D + 1)].rearrange("p (t d) -> p t d", t=NT)
                    dve.wait_ge(s.o_ps, i + 1)
                    c = base + i * 2
                    v.reciprocal(rec[:, :], o[:, :, D]).then_inc(dve_chain, 1)
                    dve.wait_ge(dve_chain, c + 1)
                    v.tensor_tensor(ON[:, :, :], o[:, :, 0:D], over(rec[:, :], D), ALU.mult).then_inc(dve_chain, 1)
                    dve.wait_ge(dve_chain, c + 2)
                    v.tensor_tensor(hb(i), hb(i), ON[:, :, :], ALU.add).then_inc(s.h_done, 1)

                norm_sum(s, 0, 0)
                norm_squares(s, 0, 0)
                norm_sum(s, 1, 1)
                norm_squares(s, 1, 1)
                low_parts(0, 0)
                if layer == 0:
                    copy_v(s, 0, 0)
                copy_k(s, keys, made, 0, 0)
                maxima(0, 0)
                norm_sum(s, 2, 0)
                norm_squares(s, 2, 0)

                def body(i, par):
                    if has(i + 3):
                        norm_sum(s, i + 3, 1 - par)
                    if has(i + 1):
                        low_parts(i + 1, 1 - par)
                        if layer == 0:
                            copy_v(s, i + 1, 1 - par)
                        copy_k(s, keys, made, i + 1, 1 - par)
                        maxima(i + 1, 1 - par)
                    if has(i + 3):
                        norm_squares(s, i + 3, 1 - par)
                    finish(i, par)

                sweep(dve, body)

            dve.wait_ge(h0_ready, NSEQ)
            attention(a0, count[0], 0)
            dve.wait_ge(a0.h_done, NSEQ)

            base = count[0] + 2 * NSEQ
            dve.wait_ge(route_in, 16)
            dve.wait_ge(experts_in, 16)

            def experts_of(i, par):
                if not known(i) or i >= 2:
                    dve.wait_ge(f0.l1_ps, i - 1)
                    dve.wait_ge(f0.h1_ready, i - 1)
                    dve.wait_ge(f0.h2_ready, i - 1)
                for g in range(NG):
                    r = dve.value_load(route_sb[0:1, bass.ds(i * NG + g, 1)], min_val=0, max_val=NEXP0 - 1)
                    ins = v.tensor_tensor(WC[:, par, g, :],
                                          WX[:, bass.ds(r, 1), :].rearrange("p a n -> p (a n)"), WS[:, :], ALU.add)
                ins.then_inc(f0.wc_ready, 1)

            def group(ap, g):
                return ap.rearrange("k (t g p) -> k g t p", t=NT, g=NG)[:, g, :, :]

            def layer1(i, par):
                dve.wait_ge(f0.l1_ps, i + 1)
                for g in range(NG):
                    ins = v.tensor_scalar(group(F2[:, par, :], g), group(bank[3][:, :], g),
                                          WC[:, par, g, WROW + HID:WROW + HID + 1], 0.0, ALU.add, ALU.max)
                ins.then_inc(f0.h2_ready, 1)

            def finish0(i, par):
                dve.wait_ge(f0.o_ps, i + 1)
                o = bank[4][:, 0:NT * D].rearrange("p (t d) -> p t d", t=NT)
                v.tensor_tensor(ON[:, :, :], o, w("bo0").unsqueeze(1).to_broadcast([P, NT, D]),
                                ALU.add).then_inc(dve_chain, 1)
                dve.wait_ge(dve_chain, i + (base + 1))
                v.tensor_tensor(hb(i), hb(i), ON[:, :, :], ALU.add).then_inc(f0.h_done, 1)

            experts_of(0, 0)
            for i in range(3):
                norm_sum(f0, i, i % 2)
                norm_squares(f0, i, i % 2)

            def ffn0(i, par):
                if has(i + 3):
                    norm_sum(f0, i + 3, 1 - par)
                if not known(i) or i >= 1:
                    layer1(i - 1, 1 - par)
                if has(i + 1):
                    experts_of(i + 1, 1 - par)
                if has(i + 3):
                    norm_squares(f0, i + 3, 1 - par)
                if not known(i) or i >= 2:
                    finish0(i - 2, par)

            sweep(dve, ffn0)
            finish0(NSEQ - 2, 0)
            layer1(NSEQ - 1, 1)
            finish0(NSEQ - 1, 1)
            dve.wait_ge(f0.h_done, NSEQ)

            attention(a1, base + NSEQ, 1)
            dve.wait_ge(a1.h_done, NSEQ)

            GATE = 7
            base1 = base + 3 * NSEQ

            def gate(i, par):
                c = base1 + i * GATE
                dve.wait_ge(f1.g_ps, i + 1)
                v.tensor_tensor(gs[:, :, :], bank[1][:, 0:NT * NEXP1].rearrange("p (t e) -> p t e", t=NT),
                                w("bg").unsqueeze(1).to_broadcast([P, NT, NEXP1]), ALU.add).then_inc(dve_chain, 1)
                dve.wait_ge(dve_chain, c + 1)
                full = [P, NT, NEXP1, NEXP1]
                other = gs[:, :, :].unsqueeze(2).to_broadcast(full)
                own = gs[:, :, :].unsqueeze(3).to_broadcast(full)
                table = [P, NT, NEXP1 * NEXP1]
                v.tensor_tensor(cge[:, :, :, :], other, own, ALU.is_ge).then_inc(dve_chain, 1)
                v.tensor_tensor(cgt[:, :, :, :], other, own, ALU.is_gt).then_inc(dve_chain, 1)
                dve.wait_ge(dve_chain, c + 3)
                for m, name in ((cge, "before"), (cgt, "after")):
                    flat = m[:, :, :, :].rearrange("p t e j -> p t (e j)")
                    v.tensor_tensor(flat, flat, w(name).unsqueeze(1).to_broadcast(table),
                                    ALU.mult).then_inc(dve_chain, 1)
                dve.wait_ge(dve_chain, c + 5)
                v.tensor_tensor(cge[:, :, :, :], cge[:, :, :, :], cgt[:, :, :, :], ALU.add).then_inc(dve_chain, 1)
                dve.wait_ge(dve_chain, c + 6)
                v.tensor_reduce(rank[:, :, :], cge[:, :, :, :], axis=AX, op=ALU.add).then_inc(dve_chain, 1)
                dve.wait_ge(dve_chain, c + 7)
                if not known(i) or i >= 1:
                    dve.wait_ge(f1.mt_ps, i)
                v.tensor_scalar(MK[:, :, D:D + NEXP1], rank[:, :, :], float(TOPK) - 0.5, -1.0, ALU.is_gt, ALU.mult)
                v.tensor_scalar(MK[:, :, D + NEXP1:D + 2 * NEXP1], rank[:, :, :], float(TOPK) - 0.5, None,
                                ALU.is_lt).then_inc(f1.mk_ready, 1)

            def copy_xh(i, par):
                dve.wait_ge(f1.x2_ready, i + 1)
                if not known(i) or i >= 2:
                    dve.wait_ge(f1.b2_ps, i - 1)
                v.tensor_copy(K2[0:D, par, :], f32(X2[0:D, par, :])).then_inc(f1.xh_ready, 1)

            def finish1(i, par):
                dve.wait_ge(f1.o_ps, i + 1)
                v.tensor_tensor(hb(i), hb(i), bank[6][:, 0:NT * D].rearrange("p (t d) -> p t d", t=NT),
                                ALU.add).then_inc(f1.h_done, 1)

            for i in range(3):
                norm_sum(f1, i, i % 2)
                norm_squares(f1, i, i % 2)
            copy_xh(0, 0)
            gate(0, 0)

            def ffn1(i, par):
                if has(i + 3):
                    norm_sum(f1, i + 3, 1 - par)
                if has(i + 1):
                    copy_xh(i + 1, 1 - par)
                    gate(i + 1, 1 - par)
                if has(i + 3):
                    norm_squares(f1, i + 3, 1 - par)
                if not known(i) or i >= 1:
                    finish1(i - 1, 1 - par)

            sweep(dve, ffn1)
            finish1(NSEQ - 1, 1)

        @block.tensor
        def _(pe):
            mm = nc.tensor.matmul

            pe.wait_ge(pack_in, 16)
            mm(bank[5][:, 0:P], w("wq0", D), w("wk0", D), start=True, stop=True)
            mm(bank[6][:, 0:D], w("wv", D), w("wo1", D), start=True, stop=True)
            mm(bank[7][:, 0:D], w("bvc", D + 1), w("wo1", D + 1), start=True, stop=True).then_inc(prod_ready, 1)

            def embed(i, par):
                pe.wait_ge(oh_ready, i + 1)
                pe.wait_ge(op_ready, i + 1)
                if not known(i) or i >= 2:
                    pe.wait_ge(h0_ready, i - 1)
                for t in range(NT):
                    o = bank[par][:, t * D:(t + 1) * D]
                    cols = slice(t * P, (t + 1) * P)
                    mm(o, OH[:, par, cols], wh("tok"), start=True, stop=False)
                    mm(o, OH[:, par, cols], wl("tok"), start=False, stop=False)
                    mm(o, OP[:, par, cols], wh("pe", NSEQ), start=False, stop=False)
                    last = mm(o, OP[:, par, cols], wl("pe", NSEQ), start=False, stop=True)
                last.then_inc(emb_ready, 1)

            sweep(pe, embed)

            def turn(s, i, par):
                pe.wait_ge(s.xs_ready, i + 1)
                for t in range(NT):
                    last = nc.tensor.transpose(bank[0][:, t * P:(t + 1) * P], f32(XS[:, par, t, :]), w("ident"))
                last.then_inc(s.xt_ready, 1)

            def attention(s, layer):
                keys = X2 if layer == 0 else KS

                def project(i, par):
                    pe.wait_ge(s.x2_ready, i + 1)
                    if not known(i) or i >= 1:
                        pe.wait_ge(s.ql_ready, i)
                    hi, lo = (AH[:, :], AL[:, :]) if layer == 0 else (wh("wq1"), wl("wq1"))
                    mm(bank[1][:, :], hi, X2[:, par, :], start=True, stop=False)
                    mm(bank[1][:, :], lo, X2[:, par, :], start=False, stop=True).then_inc(s.q_ps, 1)
                    if layer == 0:
                        return
                    mm(bank[0][:, :], wh("wk1"), X2[:, par, :], start=True, stop=False)
                    mm(bank[0][:, :], wl("wk1"), X2[:, par, :], start=False, stop=True).then_inc(s.k_ps, 1)
                    if not known(i) or i >= 1:
                        pe.wait_ge(s.max_ready, i * NT)
                    for t in range(NT):
                        o = bank[2][:, t * D:(t + 1) * D]
                        mm(o, X2[:, par, t * P:(t + 1) * P], VH[:, :], start=True, stop=False)
                        last = mm(o, X2[:, par, t * P:(t + 1) * P], VL[:, :], start=False, stop=True)
                    last.then_inc(s.v_ps, 1)

                def scores_for_max(i, par, t):
                    if t == 0:
                        pe.wait_ge(s.qh_ready, i + 1)
                        if layer == 1:
                            pe.wait_ge(s.kl_ready, i + 1)
                            pe.wait_ge(s.v_ready, i + 1)
                    if t >= 2:
                        pe.wait_ge(s.max_ready, i * NT + (t - 1))
                    elif not known(i) or i >= 1:
                        pe.wait_ge(s.max_ready, i * NT + (t - 1))
                    mm(bank[2 + t % 2][:, :], QH[:, par, t * P:(t + 1) * P], keys[:, par, :],
                       start=True, stop=True).then_inc(s.s_ps, 1)

                def spread_max(i, par):
                    pe.wait_ge(s.max_ready, i * NT + NT)
                    if not known(i) or i >= 1:
                        pe.wait_ge(s.m_ready, i)
                    for t in range(NT):
                        last = mm(bank[7][:, t * P:(t + 1) * P], nmax[:, par, t:t + 1].to_broadcast([P, P]),
                                  IR[:, :], start=True, stop=True)
                    last.then_inc(s.m_ps, 1)

                def scores(i, par):
                    pe.wait_ge(s.m_ready, i + 1)
                    pe.wait_ge(s.ql_ready, i + 1)
                    pe.wait_ge(s.k2_ready, i + 1)
                    for kt in range(NT):
                        if kt >= 2 or not known(i) or i >= 1:
                            pe.wait_ge(s.e_ready, i * NT + (kt - 1))
                        cols = slice(kt * P, (kt + 1) * P)
                        o = bank[4 + kt % 2][:, :]
                        mm(o, keys[:, par, cols], QH[:, par, :], start=True, stop=False)
                        mm(o, K2[0:D + 1, par, cols], Q2[0:D + 1, par, :], start=False, stop=True)\
                            .then_inc(s.st_ps, 1)

                def values(i, par, qt):
                    if qt == 0:
                        pe.wait_ge(s.e_ready, i * NT + NT)
                        pe.wait_ge(s.v_ready, i + 1)
                        if not known(i) or i >= 1:
                            pe.wait_ge(s.h_done, i)
                    for kt in range(NT):
                        last = mm(bank[6][:, qt * (D + 1):(qt + 1) * (D + 1)], PT[:, par, kt, qt * P:(qt + 1) * P],
                                  V1[:, par, kt, :], start=(kt == 0), stop=(kt == NT - 1))
                    if qt == NT - 1:
                        last.then_inc(s.o_ps, 1)

                turn(s, 0, 0)
                project(0, 0)
                if layer == 1:
                    pe.wait_ge(s.kl_ready, 1)
                turn(s, 1, 1)
                for t in range(NT):
                    scores_for_max(0, 0, t)

                def body(i, par):
                    nxt, far = has(i + 1), has(i + 2)
                    spread_max(i, par)
                    if nxt:
                        project(i + 1, 1 - par)
                    scores(i, par)
                    if far:
                        if layer == 1:
                            pe.wait_ge(s.kl_ready, i + 2)
                        turn(s, i + 2, par)
                    if nxt:
                        scores_for_max(i + 1, 1 - par, 0)
                        scores_for_max(i + 1, 1 - par, 1)
                    values(i, par, 0)
                    if nxt:
                        scores_for_max(i + 1, 1 - par, 2)
                    values(i, par, 1)
                    if nxt:
                        scores_for_max(i + 1, 1 - par, 3)
                    values(i, par, 2)
                    values(i, par, 3)

                sweep(pe, body)

            pe.wait_ge(prod_read, 1)
            pe.wait_ge(h0_ready, NSEQ)
            attention(a0, 0)
            pe.wait_ge(a0.h_done, NSEQ)

            def group(ap, g):
                return ap.rearrange("k (t g p) -> k g t p", t=NT, g=NG)[:, g, :, :]

            def enter0(i, par):
                pe.wait_ge(f0.x2_ready, i + 1)
                if not known(i) or i >= 1:
                    pe.wait_ge(f0.h0_ready, i)
                mm(bank[1][:, :], wh("wi"), X2[:, par, :], start=True, stop=False)
                mm(bank[1][:, :], wl("wi"), X2[:, par, :], start=False, stop=True).then_inc(f0.wi_ps, 1)

            def routed(i, par, l):
                src, dst, done = (F0, bank[2], f0.l0_ps) if l == 0 else (F1, bank[3], f0.l1_ps)
                if l == 0:
                    pe.wait_ge(f0.wc_ready, i + 1)
                    pe.wait_ge(f0.h0_ready, i + 1)
                    if not known(i) or i >= 1:
                        pe.wait_ge(f0.h1_ready, i)
                else:
                    pe.wait_ge(f0.h1_ready, i + 1)
                    if not known(i) or i >= 1:
                        pe.wait_ge(f0.h2_ready, i)
                for g in range(NG):
                    last = mm(group(dst[:, :], g), WC[:, par, g, l * WROW:l * WROW + HID],
                              group(src[:, par, :], g), start=True, stop=True)
                last.then_inc(done, 1)

            def leave0(i, par):
                pe.wait_ge(f0.h2_ready, i + 1)
                if not known(i) or i >= 1:
                    pe.wait_ge(f0.h_done, i)
                for t in range(NT):
                    last = mm(bank[4][:, t * D:(t + 1) * D], F2[:, par, t * P:(t + 1) * P], w("wo0"),
                              start=True, stop=True)
                last.then_inc(f0.o_ps, 1)

            turn(f0, 0, 0)
            enter0(0, 0)
            turn(f0, 1, 1)

            def ffn0(i, par):
                if not known(i) or i >= 1:
                    routed(i - 1, 1 - par, 1)
                if has(i + 2):
                    pe.wait_ge(f0.x2_ready, i + 2)
                    turn(f0, i + 2, par)
                if has(i + 1):
                    enter0(i + 1, 1 - par)
                if not known(i) or i >= 2:
                    leave0(i - 2, par)
                routed(i, par, 0)

            sweep(pe, ffn0)
            leave0(NSEQ - 2, 0)
            routed(NSEQ - 1, 1, 1)
            leave0(NSEQ - 1, 1)
            pe.wait_ge(f0.h_done, NSEQ)

            attention(a1, 1)
            pe.wait_ge(a1.h_done, NSEQ)

            def gate_scores(i, par):
                pe.wait_ge(f1.x2_ready, i + 1)
                if not known(i) or i >= 1:
                    pe.wait_ge(f1.mk_ready, i)
                for t in range(NT):
                    o = bank[1][:, t * NEXP1:(t + 1) * NEXP1]
                    mm(o, X2[:, par, t * P:(t + 1) * P], wh("wg"), start=True, stop=False)
                    last = mm(o, X2[:, par, t * P:(t + 1) * P], wl("wg"), start=False, stop=True)
                last.then_inc(f1.g_ps, 1)

            def turn_masks(i, par):
                pe.wait_ge(f1.mk_ready, i + 1)
                if not known(i) or i >= 1:
                    pe.wait_ge(f1.m2_ready, i)
                for t in range(NT):
                    last = nc.tensor.transpose(bank[2][:, t * P:(t + 1) * P], MK[:, t, :], w("ident"))
                last.then_inc(f1.mt_ps, 1)

            def up(i, par, e):
                if e == 0:
                    pe.wait_ge(f1.xh_ready, i + 1)
                    pe.wait_ge(f1.m2_ready, i + 1)
                if e >= 3:
                    pe.wait_ge(f1.gelu_ready, i * NEXP1 + (e - 2))
                elif not known(i) or i >= 1:
                    pe.wait_ge(f1.gelu_ready, i * NEXP1)
                a = at["w1"][0] + e * HID
                o = bank[3 + e % 3][:, :]
                mm(o, WH[:, a:a + HID], X2[:, par, :], start=True, stop=False)
                mm(o, WL[0:D + 2 * NEXP1, a:a + HID], K2[0:D + 2 * NEXP1, par, :], start=False, stop=True)\
                    .then_inc(f1.u_ps, 1)

            def down_bias(i, par):
                if not known(i) or i >= 1:
                    pe.wait_ge(f1.h_done, i)
                rows = D + 2 * NEXP1
                for t in range(NT):
                    o = bank[6][:, t * D:(t + 1) * D]
                    masks = K2[0:rows, par, t * P:(t + 1) * P]
                    mm(o, masks, wh("b2", rows), start=(t == 0), stop=False, skip_group_check=True)
                    last = mm(o, masks, wl("b2", rows), start=False, stop=False, skip_group_check=True)
                last.then_inc(f1.b2_ps, 1)

            def down(i, par, t, part):
                o = bank[6][:, t * D:(t + 1) * D]
                cols = slice(t * P, (t + 1) * P)
                if part == 0 and t == 0:
                    pe.wait_ge(f1.gelu_ready, i * NEXP1 + NEXP1)
                some = NEXP1 // 2
                for e in range(part * some, (part + 1) * some):
                    a = at["w2"][0] + e * D
                    last = mm(o, G[:, par, e, cols], W[:, a:a + D], start=False, stop=(e == NEXP1 - 1),
                              skip_group_check=True)
                if part == 1 and t == NT - 1:
                    last.then_inc(f1.o_ps, 1)

            turn(f1, 0, 0)
            gate_scores(0, 0)
            turn(f1, 1, 1)
            turn_masks(0, 0)

            def ffn1(i, par):
                for e in range(NEXP1):
                    up(i, par, e)
                    if not known(i) or i >= 1:
                        if e == 0:
                            down_bias(i - 1, 1 - par)
                        down(i - 1, 1 - par, e // 2, e % 2)
                    if e == 0 and has(i + 1):
                        gate_scores(i + 1, 1 - par)
                    if e == NEXP1 - 2 and has(i + 1):
                        turn_masks(i + 1, 1 - par)
                if has(i + 2):
                    pe.wait_ge(f1.x2_ready, i + 2)
                    turn(f1, i + 2, par)

            sweep(pe, ffn1)
            down_bias(NSEQ - 1, 1)
            for t in range(NT):
                for part in range(2):
                    down(NSEQ - 1, 1, t, part)


def kernel(**inputs):
    import concourse.bacc as bacc
    from concourse.bass_utils import run_bass_kernel_spmd

    x = {k: np.asarray(v) for k, v in inputs.items()}
    at, width = columns()
    pack = np.zeros((P, width), np.float32)

    def put(name, value, row=0):
        value = np.asarray(value)
        if value.ndim == 1:
            value = value[:, None]
        a = at[name][0]
        pack[row:row + value.shape[0], a:a + value.shape[1]] = value

    def twice(m):
        return np.concatenate([m, m], 0)

    def wide(m):
        return np.concatenate([m, m], 1)

    put("wq0", wide(x["L0_attn_Wq"]))
    put("wk0", wide(x["L0_attn_Wk"]))
    put("wq1", twice(wide(x["L1_attn_Wq"].T)))
    put("wk1", twice(wide(x["L1_attn_Wk"].T)))
    put("bq", twice(x["L1_attn_bq"][:, None]))
    put("bk", twice(x["L1_attn_bk"][:, None]))
    put("wv", wide(x["L1_attn_Wv"]))
    put("wo1", x["L1_attn_Wo"].T)
    put("wo1", x["L1_attn_bo"][None, :], D)
    put("bvc", np.broadcast_to(x["L1_attn_bv"][:, None], (D, P)))
    put("bvc", np.ones((1, P), np.float32), D)
    put("wi", twice(x["L0_ffn_Wi"].T))
    put("bi", x["L0_ffn_bi"])
    put("wo0", x["L0_ffn_Wo"].T)
    put("bo0", np.broadcast_to(x["L0_ffn_bo"][None, :], (P, D)))
    put("w1", twice(x["L1_ffn_W1"].transpose(1, 0, 2).reshape(D, NEXP1 * HID)))
    put("b1", x["L1_ffn_b1"].T)
    put("w2", x["L1_ffn_W2"].transpose(1, 0, 2).reshape(HID, NEXP1 * D))
    put("b2", x["L1_ffn_b2"], D + NEXP1)
    put("wg", twice(x["L1_ffn_Wg"]))
    put("bg", np.broadcast_to(x["L1_ffn_bg"][None, :], (P, NEXP1)))
    put("tok", x["L0_tok_token_W"])
    put("pe", x["L0_tok_pe"][:NSEQ])
    ws = np.zeros((P, NLAY0, WROW), np.float32)
    ws[:, :, :HID] = x["L0_ffn_Ws"][:, 0].transpose(2, 0, 1)
    ws[:, :, HID] = x["L0_ffn_bs"][:, 0].T
    put("ws", ws.reshape(P, NLAY0 * WROW))
    experts = np.zeros((P, NEXP0, NLAY0, WROW), np.float32)
    experts[:, :, :, :HID] = x["L0_ffn_Wr"].transpose(3, 1, 0, 2)
    experts[:, :, :, HID] = x["L0_ffn_br"].transpose(2, 1, 0)
    put("ident", np.eye(P, dtype=np.float32))
    put("iota", np.arange(P, dtype=np.float32))
    put("steps", np.broadcast_to(np.repeat(np.arange(NSEQ, dtype=np.float32), NT), (P, NSEQ * NT)))
    e, j = np.meshgrid(np.arange(NEXP1), np.arange(NEXP1), indexing="ij")
    put("before", np.broadcast_to((j < e).astype(np.float32).reshape(1, -1), (P, NEXP1 ** 2)))
    put("after", np.broadcast_to((j >= e).astype(np.float32).reshape(1, -1), (P, NEXP1 ** 2)))
    sel = np.zeros((NEXP1, NEXP1, HID), np.float32)
    for k in range(NEXP1):
        sel[k, k] = -OFF
    put("sel", sel.reshape(NEXP1, -1), D)

    nc = bacc.Bacc("TRN2", target_bir_lowering=False, num_devices=1)
    arrays = {
        "tokens": np.ascontiguousarray(x["x"]),
        "route": np.ascontiguousarray(x["L0_ffn_route_id"].reshape(1, -1)),
        "pack": pack,
        "experts": experts.reshape(P, NEXP0, NLAY0 * WROW),
    }
    args = [nc.dram_tensor(n, a.shape, mybir.dt.from_np(a.dtype), kind="ExternalInput").ap()
            for n, a in arrays.items()]
    out = nc.dram_tensor("out", (NSEQ, SEQ, D), F32, kind="ExternalOutput").ap()
    pos = nc.dram_tensor("pos", (NSEQ, SEQ), F32, kind="Internal").ap()
    tower_kernel(nc, *args, out, pos)
    result = run_bass_kernel_spmd(nc, [arrays], core_ids=[0])
    return result.results[0]["out"]
```

```python
from contextlib import ExitStack

import numpy as np

import concourse.bass as bass
from concourse import mybir

F32 = mybir.dt.float32
F32R = mybir.dt.float32r
BF16 = mybir.dt.bfloat16
I32 = mybir.dt.int32
ALU = mybir.AluOpType
ACT = mybir.ActivationFunctionType
AX = mybir.AxisListType.X

P = 128
NSEQ, SEQ, D = 32, 512, 64
NT = SEQ // P
HID = 128
NEXP0, NLAY0 = 16, 2
NEXP1, TOPK = 8, 2
VOCAB = 128
SEP_ID, PAD_ID = 13, 1
EPS = 1e-5
LOAD = 4
LAG = 6
CONSTS = 6
SCALE = D ** -0.5
GROUP = SEQ * NSEQ // 64
NG = SEQ // GROUP
WROW = HID + 1
NONE, TAKEN = -3e38, 3e38
OFF = -(2.0 ** 100)

SPLIT = [("wq1", P), ("wk1", P), ("wi", HID), ("w1", NEXP1 * HID), ("wg", NEXP1), ("b2", D),
         ("w2", NEXP1 * D)]
PLAIN = [("tok", D), ("pe", D), ("sel", NEXP1 * HID), ("wq0", P), ("wk0", P), ("wv", P), ("wo1", D), ("bvc", P),
         ("wo0", D), ("b1", NEXP1), ("bi", 1), ("bq", 1), ("bk", 1),
         ("bo0", 1), ("bg", NEXP1), ("ident", P), ("iota", 1), ("steps", NSEQ * NT),
         ("ws", NLAY0 * WROW)]


def columns():
    at, n = {}, 0
    for name, width in SPLIT + PLAIN:
        at[name] = (n, n + width)
        n += width
    return at, n


class NormSignals:

    def __init__(self, sem, tag):
        self.xh_done = sem(f"{tag}_xh_done")
        self.sqsum_ready = sem(f"{tag}_sqsum_ready")
        self.sum_ready = sem(f"{tag}_sum_ready")
        self.xc_ready = sem(f"{tag}_xc_ready")
        self.sq_ready = sem(f"{tag}_sq_ready")
        self.var_ready = sem(f"{tag}_var_ready")
        self.xs_ready = sem(f"{tag}_xs_ready")
        self.xt_ready = sem(f"{tag}_xt_ready")
        self.x2_ready = sem(f"{tag}_x2_ready")
        self.h_done = sem(f"{tag}_h_done")


class AttentionSignals(NormSignals):

    def __init__(self, sem, tag):
        super().__init__(sem, tag)
        self.k2_ready = sem(f"{tag}_k2_ready")
        self.v_ready = sem(f"{tag}_v_ready")
        self.q_ps = sem(f"{tag}_q_ps")
        self.qh_ready = sem(f"{tag}_qh_ready")
        self.ql_ready = sem(f"{tag}_ql_ready")
        self.s_ps = sem(f"{tag}_s_ps")
        self.max_ready = sem(f"{tag}_max_ready")
        self.m_ps = sem(f"{tag}_m_ps")
        self.m_ready = sem(f"{tag}_m_ready")
        self.st_ps = sem(f"{tag}_st_ps")
        self.e_ready = sem(f"{tag}_e_ready")
        self.o_ps = sem(f"{tag}_o_ps")
        self.ot_ready = sem(f"{tag}_ot_ready")
        self.back_ps = sem(f"{tag}_back_ps")
        self.k_ps = sem(f"{tag}_k_ps")
        self.kh_ready = sem(f"{tag}_kh_ready")
        self.kl_ready = sem(f"{tag}_kl_ready")
        self.v_ps = sem(f"{tag}_v_ps")
        self.vh_done = sem(f"{tag}_vh_done")


class RoutedSignals(NormSignals):

    def __init__(self, sem, tag):
        super().__init__(sem, tag)
        self.wc_ready = sem(f"{tag}_wc_ready")
        self.wi_ps = sem(f"{tag}_wi_ps")
        self.h0_ready = sem(f"{tag}_h0_ready")
        self.l0_ps = sem(f"{tag}_l0_ps")
        self.h1_ready = sem(f"{tag}_h1_ready")
        self.l1_ps = sem(f"{tag}_l1_ps")
        self.h2_ready = sem(f"{tag}_h2_ready")
        self.o_ps = sem(f"{tag}_o_ps")
        self.ot_ready = sem(f"{tag}_ot_ready")
        self.back_ps = sem(f"{tag}_back_ps")


class MixtureSignals(NormSignals):

    def __init__(self, sem, tag):
        super().__init__(sem, tag)
        self.xh_ready = sem(f"{tag}_xh_ready")
        self.g_ps = sem(f"{tag}_g_ps")
        self.mk_ready = sem(f"{tag}_mk_ready")
        self.b2_ps = sem(f"{tag}_b2_ps")
        self.mt_ps = sem(f"{tag}_mt_ps")
        self.m2_ready = sem(f"{tag}_m2_ready")
        self.u_ps = sem(f"{tag}_u_ps")
        self.gelu_ready = sem(f"{tag}_gelu_ready")
        self.high_ready = sem(f"{tag}_high_ready")
        self.low_dve = sem(f"{tag}_low_dve")
        self.low_pool = sem(f"{tag}_low_pool")
        self.down_ps = sem(f"{tag}_down_ps")
        self.h_half = sem(f"{tag}_h_half")
        self.o_ps = sem(f"{tag}_o_ps")
        self.ot_ready = sem(f"{tag}_ot_ready")
        self.back_ps = sem(f"{tag}_back_ps")


def sweep(eng, body, first=4, last=NSEQ - 4):
    for i in range(first):
        body(i, i % 2)
    with eng.Fori(first // 2, last // 2) as pair:
        body(pair * 2, 0)
        body(pair * 2 + 1, 1)
    for i in range(last, NSEQ):
        body(i, i % 2)


def known(i):
    return isinstance(i, int)


def has(i):
    return not known(i) or i < NSEQ


def tower_kernel(nc, tokens, route, pack, experts, out, pos_dram):
    at, width = columns()
    n_split = at[SPLIT[-1][0]][1]

    with ExitStack() as ctx:
        def sb(name, shape, dt=F32):
            return ctx.enter_context(nc.sbuf_tensor(name, shape, dt))

        def ps(name):
            return ctx.enter_context(nc.psum_tensor(name, [P, 512], F32))

        def sem(name):
            return ctx.enter_context(nc.semaphore(name))

        H = sb("H", [P, NSEQ, NT, D])
        W = sb("W", [P, width])
        WH = sb("WH", [P, n_split], F32R)
        WL = sb("WL", [P, n_split], F32R)
        WR = sb("WR", [P, 2, NG, NLAY0 * WROW])
        WS = sb("WS", [P, NLAY0 * WROW])
        WC = sb("WC", [P, 2, NG, NLAY0 * WROW])
        AH = sb("AH", [P, P], F32R)
        AL = sb("AL", [P, P], F32R)
        VHL = sb("VHL", [P, 2 * D], F32R)
        B2 = sb("B2", [P, 2 * D], F32R)
        GHL = sb("GHL", [P, 2 * NEXP1], F32R)
        T3 = sb("T3", [P, 2, 3, D], BF16)
        rest = sb("rest", [P, 2, D])
        VB = sb("VB", [P, D])
        IR = sb("IR", [P, P], F32R)
        half = sb("half", [P, NT])
        ninv = sb("ninv", [P, NT])
        route_sb = sb("route_sb", [1, NSEQ * NG], I32)

        tk = sb("tk", [P, NSEQ * NT], I32)
        sc = [sb(f"sc{k}", [P, NSEQ * NT]) for k in range(8)]
        posb = sb("posb", [NSEQ, 2, LOAD, SEQ])
        OH = sb("OH", [P, 2, SEQ], BF16)
        OP = sb("OP", [NSEQ, 2, SEQ], BF16)

        stat = sb("stat", [P, 2, 4, NT])
        var = sb("var", [P, NT])
        XC = sb("XC", [P, 2, NT, D])
        SQ = sb("SQ", [P, NT, D])
        XN = sb("XN", [P, 2, NT, D])
        XS = sb("XS", [P, 2, NT, 2 * D], F32R)
        X2 = sb("X2", [P, 2, SEQ], F32R)
        KS = sb("KS", [P, 2, SEQ], F32R)
        K2 = sb("K2", [P, 2, SEQ], F32R)
        QH = sb("QH", [P, 2, SEQ], F32R)
        Q2 = sb("Q2", [P, 2, SEQ], F32R)
        V1 = sb("V1", [P, 2, NT, D + 1])
        PT = sb("PT", [P, 2, NT, SEQ])
        nmax = sb("nmax", [P, 2, NT], F32R)
        rec = sb("rec", [P, NT])
        ON = sb("ON", [P, NT, D])
        OT = sb("OT", [P, 2, SEQ])
        F0 = sb("F0", [P, 2, SEQ])
        F1 = sb("F1", [P, 2, SEQ])
        F2 = sb("F2", [P, 2, SEQ])
        idb = PT[:, :, :, :].bitcast(I32)
        G = PT[:, :, :, :].rearrange("p a t n -> p (a t) n")
        GH = sb("GH", [P, NEXP1, SEQ], F32R)
        GL = sb("GL", [P, NEXP1, SEQ], F32R)
        W2 = sb("W2", [P, NEXP1, 2 * D], F32R)
        gs = sb("gs", [P, NT, NEXP1])
        g16 = sb("g16", [P, NT, 2 * NEXP1])
        top = sb("top", [P, NT, NEXP1])
        took = sb("took", [P, NT, 2 * NEXP1])
        MK = sb("MK", [P, NT, P])

        bank = [ps(f"bank{k}") for k in range(8)]

        def w(name, rows=P):
            a, b = at[name]
            return W[0:rows, a:b]

        def wh(name, rows=P):
            a, b = at[name]
            return WH[0:rows, a:b]

        def wl(name, rows=P):
            a, b = at[name]
            return WL[0:rows, a:b]

        def f32(ap):
            return ap.bitcast(F32)

        def hb(i):
            return H[:, bass.ds(i, 1), :, :].rearrange("p a t d -> p (a t) d")

        def over(ap, n):
            return ap.unsqueeze(2).to_broadcast([P, NT, n])

        tok_in, pack_in, route_in = sem("tok_in"), sem("pack_in"), sem("route_in")
        routed_in = [sem("routed_in0"), sem("routed_in1")]
        pos_out, ids_in, pos_in, stored = sem("pos_out"), [sem("ids_in0"), sem("ids_in1")], [sem("pos_in0"), sem("pos_in1")], sem("stored")
        dve_chain = sem("dve_chain")
        mean_done, sigma_done, xn_done = sem("mean_done"), sem("sigma_done"), sem("xn_done")
        consts_set, parts_ready, prod_ready, prod_read = (
            sem("consts_set"), sem("parts_ready"), sem("prod_ready"), sem("prod_read"))
        oh_ready, op_ready, emb_ready, h0_ready = sem("oh_ready"), sem("op_ready"), sem("emb_ready"), sem("h0_ready")

        a0, a1 = AttentionSignals(sem, "a0"), AttentionSignals(sem, "a1")
        f0, f1 = RoutedSignals(sem, "f0"), MixtureSignals(sem, "f1")

        block = ctx.enter_context(nc.Block())

        @block.sync
        def _(sp):
            sp.dma_start(tk[:, :].rearrange("p (s t) -> p s t", t=NT),
                         tokens.rearrange("s (p t) -> p s t", t=NT)).then_inc(tok_in, 16)
            sp.dma_start(W[:, :], pack).then_inc(pack_in, 16)
            sp.dma_start(route_sb[:, :], route).then_inc(route_in, 16)
            sp.wait_ge(parts_ready, 1)
            sp.dma_start(pos_dram.rearrange("s (p t) -> p s t", t=NT),
                         sc[7][:, :].rearrange("p (s t) -> p s t", t=NT)).then_inc(pos_out, 16)
            sp.wait_ge(pos_out, 16)

            def load_ids(k, par):
                if k >= 2:
                    sp.wait_ge(op_ready, (k - 1) * LOAD)
                rows = slice(k * LOAD, (k + 1) * LOAD)
                sp.dma_start(idb[:, par, :, :],
                             tokens[rows, :].unsqueeze(0).to_broadcast([P, LOAD, SEQ])).then_inc(ids_in[par], 16)
                sp.dma_start(posb[:, par, :, :],
                             pos_dram[rows, :].unsqueeze(0).to_broadcast([NSEQ, LOAD, SEQ])).then_inc(pos_in[par], 16)

            for k in range(NSEQ // LOAD):
                load_ids(k, k % 2)

            def load_experts(i, par):
                if not known(i) or i >= 2:
                    sp.wait_ge(f0.wc_ready, i - 1)
                for g in range(NG):
                    expert = sp.value_load(route_sb[0:1, bass.ds(i * NG + g, 1)], min_val=0, max_val=NEXP0 - 1)
                    sp.dma_start(WR[:, par, g, :],
                                 experts[bass.ds(expert, 1), :, :].rearrange("a p n -> p (a n)"))\
                        .then_inc(routed_in[par], 16)

            sp.wait_ge(route_in, 16)
            sweep(sp, load_experts)
            out_rows = out.rearrange("b (p t) d -> p b (t d)", t=NT)

            def store(i, par):
                sp.wait_ge(f1.h_done, i + 1)
                sp.dma_start(out_rows[:, bass.ds(i, 1), :],
                             H[:, bass.ds(i, 1), :, :].rearrange("p a t d -> p a (t d)")).then_inc(stored, 16)

            sweep(sp, store)
            sp.wait_ge(stored, 16 * NSEQ)

        @block.gpsimd
        def _(pool):
            pl = nc.gpsimd

            pl.memset(half[:, :], -0.5).then_inc(consts_set, 1)
            pl.memset(ninv[:, :], -1.0 / D).then_inc(consts_set, 1)
            pl.memset(V1[:, :, :, :], 1.0).then_inc(consts_set, 1)
            pl.memset(f32(K2[:, :, :]), 1.0).then_inc(consts_set, 1)
            pl.memset(MK[:, :, :], 0.0).then_inc(consts_set, 1)
            pl.memset(OT[:, :, :], 0.0).then_inc(consts_set, 1)

            pool.wait_ge(consts_set, CONSTS)

            def norm_centre(s, phase, i, par):
                pool.wait_ge(s.sum_ready, i + 1)
                pl.tensor_tensor(stat[:, par, 1, :], stat[:, par, 0, :], ninv[:, :], ALU.mult).then_inc(mean_done, 1)
                pool.wait_ge(mean_done, phase * NSEQ + i + 1)
                if not known(i) or i >= 2:
                    pool.wait_ge(s.var_ready, i - 1)
                pl.tensor_tensor(XC[:, par, :, :], hb(i), over(stat[:, par, 1, :], D), ALU.add)\
                    .then_inc(s.xc_ready, 1)

            def norm_scale(s, phase, i, par):
                pool.wait_ge(s.var_ready, i + 1)
                pl.tensor_tensor(stat[:, par, 3, :], stat[:, par, 2, :], half[:, :], ALU.pow).then_inc(sigma_done, 1)
                pool.wait_ge(sigma_done, phase * NSEQ + i + 1)
                scale = over(stat[:, par, 3, :], D)
                pl.tensor_tensor(XN[:, par, :, :], XC[:, par, :, :], scale, ALU.mult).then_inc(xn_done, 1)
                if not known(i) or i >= 2:
                    pool.wait_ge(s.xt_ready, i - 1)
                pl.tensor_tensor(XS[:, par, :, 0:D], XC[:, par, :, :], scale, ALU.mult).then_inc(s.xh_done, 1)
                pool.wait_ge(xn_done, phase * NSEQ + i + 1)
                pool.wait_ge(s.xh_done, i + 1)
                pl.tensor_tensor(XS[:, par, :, D:2 * D], XN[:, par, :, :], f32(XS[:, par, :, 0:D]),
                                 ALU.subtract).then_inc(s.xs_ready, 1)

            def first_norms(s, phase):
                norm_centre(s, phase, 0, 0)
                for i in range(3):
                    norm_centre(s, phase, i + 1, 1 - i % 2)
                    norm_scale(s, phase, i, i % 2)

            def norms(s, phase):
                first_norms(s, phase)

                def body(i, par):
                    if has(i + 4):
                        norm_centre(s, phase, i + 4, par)
                    if has(i + 3):
                        norm_scale(s, phase, i + 3, 1 - par)

                sweep(pool, body)

            pool.wait_ge(h0_ready, NSEQ)
            norms(a0, 0)
            pool.wait_ge(a0.h_done, NSEQ)
            norms(f0, 1)
            pool.wait_ge(f0.h_done, NSEQ)
            norms(a1, 2)
            pool.wait_ge(a1.h_done, NSEQ)
            first_norms(f1, 3)

            def low(i, e):
                pool.wait_ge(f1.high_ready, i * NEXP1 + (e + 1))
                pl.tensor_tensor(GL[:, e, :], G[:, e, :], f32(GH[:, e, :]), ALU.subtract).then_inc(f1.low_pool, 1)

            def ffn1(i, par):
                if has(i + 4):
                    norm_centre(f1, 3, i + 4, par)
                low(i, 1)
                low(i, 3)
                low(i, 5)
                low(i, 7)
                if has(i + 3):
                    norm_scale(f1, 3, i + 3, 1 - par)

            sweep(pool, ffn1)

        @block.scalar
        def _(act):
            sc_ = nc.scalar

            def embed(i, par):
                act.wait_ge(emb_ready, i + 1)
                sc_.activation(hb(i), bank[par][:, 0:NT * D].rearrange("p (t d) -> p t d", t=NT),
                               ACT.Copy).then_inc(h0_ready, 1)

            sweep(act, embed)

            def evac_x(s, i, par):
                act.wait_ge(s.xt_ready, i + 1)
                if s is a0 and (not known(i) or i >= 2):
                    act.wait_ge(s.st_ps, i * NT - 4)
                sc_.activation(X2[:, par, :], bank[0][:, :], ACT.Copy).then_inc(s.x2_ready, 1)

            def evac_o(s, src, rows, i, par):
                if s is f1:
                    act.wait_ge(s.down_ps, i * NEXP1 + NEXP1)
                else:
                    act.wait_ge(s.o_ps, i + 1)
                if not known(i) or i >= 2:
                    act.wait_ge(s.back_ps, i - 1)
                if s is f0:
                    ins = sc_.activation(OT[0:rows, par, :], src[0:rows, :], ACT.Identity, bias=w("bo0", D))
                else:
                    ins = sc_.activation(OT[0:rows, par, :], src[0:rows, :], ACT.Copy)
                ins.then_inc(s.ot_ready, 1)

            def attention(s, layer):
                def evac_q(i, par):
                    act.wait_ge(s.q_ps, i + 1)
                    if layer == 0:
                        sc_.activation(QH[:, par, :], bank[1][:, :], ACT.Copy).then_inc(s.qh_ready, 1)
                    else:
                        sc_.activation(QH[:, par, :], bank[1][:, :], ACT.Identity,
                                       bias=w("bq")).then_inc(s.qh_ready, 1)
                        act.wait_ge(s.k_ps, i + 1)
                        sc_.activation(KS[:, par, :], bank[3][:, :], ACT.Identity,
                                       bias=w("bk")).then_inc(s.kh_ready, 1)

                evac_x(s, 0, 0)
                evac_q(0, 0)
                evac_x(s, 1, 1)

                def body(i, par):
                    if not known(i) or i >= 1:
                        evac_o(s, bank[6], D + 1, i - 1, 1 - par)
                    act.wait_ge(s.m_ps, i + 1)
                    sc_.activation(Q2[D:D + 1, par, :], bank[7][D:D + 1, :], ACT.Copy).then_inc(s.m_ready, 1)
                    if has(i + 1):
                        evac_q(i + 1, 1 - par)
                    for kt in range(NT):
                        act.wait_ge(s.st_ps, i * NT + (kt + 1))
                        if kt == 0 and (not known(i) or i >= 2):
                            act.wait_ge(s.o_ps, i - 1)
                        sc_.activation(PT[:, par, kt, :], bank[4 + kt % 2][:, :], ACT.Exp,
                                       scale=SCALE).then_inc(s.e_ready, 1)
                    if has(i + 2):
                        evac_x(s, i + 2, par)

                sweep(act, body)
                evac_o(s, bank[6], D + 1, NSEQ - 1, 1)

            act.wait_ge(pack_in, 16)
            attention(a0, 0)
            act.wait_ge(a0.h_done, NSEQ)

            def ffn0_in(i, par):
                act.wait_ge(f0.wi_ps, i + 1)
                sc_.activation(F0[:, par, :], bank[1][:, :], ACT.Relu, bias=w("bi")).then_inc(f0.h0_ready, 1)

            evac_x(f0, 0, 0)
            ffn0_in(0, 0)
            evac_x(f0, 1, 1)

            def ffn0(i, par):
                if has(i + 2):
                    evac_x(f0, i + 2, par)
                if has(i + 1):
                    ffn0_in(i + 1, 1 - par)
                act.wait_ge(f0.l0_ps, i + 1)
                act.wait_ge(f0.wc_ready, i + 1)
                for g in range(NG):
                    ins = sc_.activation(group(F1[:, par, :], g), group(bank[2][:, :], g), ACT.Relu,
                                         bias=WC[:, par, g, HID:HID + 1])
                ins.then_inc(f0.h1_ready, 1)
                if not known(i) or i >= 2:
                    evac_o(f0, bank[4], D, i - 2, par)

            def group(ap, g):
                return ap.rearrange("k (t g p) -> k g t p", t=NT, g=NG)[:, g, :, :]

            sweep(act, ffn0)
            evac_o(f0, bank[4], D, NSEQ - 2, 0)
            evac_o(f0, bank[4], D, NSEQ - 1, 1)
            act.wait_ge(f0.h_done, NSEQ)
            attention(a1, 1)
            act.wait_ge(a1.h_done, NSEQ)

            def masks(i, par):
                act.wait_ge(f1.mt_ps, i + 1)
                if not known(i) or i >= 2:
                    act.wait_ge(f1.b2_ps, i - 1)
                sc_.activation(K2[D:D + 2 * NEXP1, par, :], bank[2][D:D + 2 * NEXP1, :],
                               ACT.Copy).then_inc(f1.m2_ready, 1)

            evac_x(f1, 0, 0)
            evac_x(f1, 1, 1)
            masks(0, 0)

            def gelu(i, e):
                act.wait_ge(f1.u_ps, i * NEXP1 + (e + 1))
                if not known(i) or i >= 1:
                    split = f1.low_dve if e % 2 == 0 else f1.low_pool
                    act.wait_ge(split, i * 4 + (e // 2 - 3))
                sc_.activation(G[:, e, :], bank[3 + e % 2][:, :], ACT.Gelu,
                               bias=W[:, at["b1"][0] + e:at["b1"][0] + e + 1]).then_inc(f1.gelu_ready, 1)

            def ffn1(i, par):
                for e in range(5):
                    gelu(i, e)
                gelu(i, 5)
                if has(i + 1):
                    masks(i + 1, 1 - par)
                if not known(i) or i >= 1:
                    evac_o(f1, bank[6 - par], P, i - 1, 1 - par)
                gelu(i, 6)
                gelu(i, 7)
                if has(i + 2):
                    evac_x(f1, i + 2, par)

            sweep(act, ffn1)
            evac_o(f1, bank[6], P, NSEQ - 1, 1)

        @block.vector
        def _(dve):
            v = nc.vector
            count = [0]

            def link(ins):
                count[0] += 1
                ins.then_inc(dve_chain, 1)
                dve.wait_ge(dve_chain, count[0])

            dve.wait_ge(tok_in, 16)
            sep, pad, run, all_pad, t0, t1, skip, pos = (x[:, :] for x in sc)
            link(v.tensor_scalar(sep, tk[:, :], float(SEP_ID), None, ALU.is_equal))
            link(v.tensor_scalar(pad, tk[:, :], float(PAD_ID), None, ALU.is_equal))
            link(v.tensor_copy(all_pad, pad))
            dist = 1
            while dist < NSEQ:
                k = dist * NT
                link(v.tensor_tensor(t0[:, k:], all_pad[:, k:], sep[:, :-k], ALU.mult))
                link(v.tensor_tensor(t1[:, k:], all_pad[:, k:], all_pad[:, :-k], ALU.mult))
                link(v.tensor_tensor(sep[:, k:], sep[:, k:], t0[:, k:], ALU.max))
                link(v.tensor_copy(all_pad[:, k:], t1[:, k:]))
                dist *= 2
            link(v.memset(skip[:, 0:NT], 0.0))
            link(v.tensor_tensor(skip[:, NT:], pad[:, NT:], sep[:, :-NT], ALU.mult))
            link(v.memset(run[:, 0:NT], 0.0))
            link(v.tensor_copy(run[:, NT:], skip[:, :-NT]))
            dist = 1
            while dist < NSEQ:
                k = dist * NT
                link(v.tensor_tensor(t0[:, k:], run[:, k:], run[:, :-k], ALU.add))
                link(v.tensor_copy(run[:, k:], t0[:, k:]))
                dist *= 2
            dve.wait_ge(pack_in, 16)
            link(v.tensor_tensor(pos, w("steps"), run, ALU.subtract))
            link(v.scalar_tensor_tensor(pos, skip, -2.0 * NSEQ, pos, ALU.mult, ALU.add))
            v.tensor_copy(sc[7][:, :], pos).then_inc(parts_ready, 1)

            link(v.memset(w("tok", 1), 0.0))
            a = at["tok"][0]
            tables = W[:, a:a + 2 * D].rearrange("p (a d) -> p a d", a=2)
            link(v.tensor_copy(T3[:, :, 0, :], tables))
            link(v.tensor_tensor(rest[:, :, :], tables, T3[:, :, 0, :], ALU.subtract))
            link(v.tensor_copy(T3[:, :, 1, :], rest[:, :, :]))
            link(v.tensor_tensor(T3[:, :, 2, :], rest[:, :, :], T3[:, :, 1, :], ALU.subtract))
            link(v.tensor_copy(WH[:, :], W[:, 0:n_split]))
            link(v.tensor_tensor(WL[:, :], W[:, 0:n_split], f32(WH[:, :]), ALU.subtract))
            link(v.tensor_copy(WL[D:P, at["w1"][0]:at["w1"][1]], W[D:P, at["sel"][0]:at["sel"][1]]))
            link(v.tensor_copy(IR[:, :], w("ident")))
            v.tensor_copy(WS[:, :], w("ws")).then_inc(parts_ready, 1)
            dve.wait_ge(parts_ready, 2)
            for l in range(NLAY0):
                link(v.tensor_tensor(WS[:, l * WROW:l * WROW + HID], WS[:, l * WROW:l * WROW + HID],
                                     w("ident"), ALU.add))
            dve.wait_ge(prod_ready, 1)
            link(v.tensor_copy(AH[:, :], bank[5][:, 0:P]))
            link(v.tensor_tensor(AL[:, :], bank[5][:, 0:P], f32(AH[:, :]), ALU.subtract))
            link(v.tensor_copy(VHL[:, 0:D], bank[6][:, 0:D]))
            link(v.tensor_tensor(VHL[:, D:2 * D], bank[6][:, 0:D], f32(VHL[:, 0:D]), ALU.subtract))
            link(v.tensor_copy(GHL[:, 0:NEXP1], f32(wh("wg"))))
            link(v.tensor_copy(GHL[:, NEXP1:2 * NEXP1], f32(wl("wg"))))
            for k, part in enumerate((wh, wl)):
                link(v.tensor_copy(B2[:, k * D:(k + 1) * D], f32(part("b2"))))
                link(v.tensor_copy(W2[:, :, k * D:(k + 1) * D],
                                   f32(part("w2")).rearrange("p (e d) -> p e d", e=NEXP1)))
            v.tensor_copy(VB[:, :], bank[7][:, 0:D]).then_inc(prod_read, 1)

            def one_hots(i, par):
                at_ = (i // LOAD) % 2, i % LOAD
                if i % LOAD == 0:
                    dve.wait_ge(ids_in[at_[0]], 16 * (i // (2 * LOAD) + 1))
                    dve.wait_ge(pos_in[at_[0]], 16 * (i // (2 * LOAD) + 1))
                if i >= 2:
                    dve.wait_ge(emb_ready, i - 1)
                v.tensor_scalar(OH[:, par, :].rearrange("k (t p) -> k t p", t=NT),
                                idb[:, at_[0], at_[1], :].rearrange("k (p t) -> k t p", t=NT),
                                w("iota"), None, ALU.is_equal).then_inc(oh_ready, 1)
                v.tensor_scalar(OP[:, par, :].rearrange("k (t p) -> k t p", t=NT),
                                posb[:, at_[0], at_[1], :].rearrange("k (p t) -> k t p", t=NT),
                                w("iota", NSEQ), None, ALU.is_equal).then_inc(op_ready, 1)

            for i in range(NSEQ):
                one_hots(i, i % 2)

            def norm_sum(s, i, par):
                v.tensor_reduce(stat[:, par, 0, :], hb(i), axis=AX, op=ALU.add).then_inc(s.sum_ready, 1)

            def norm_squares(s, i, par):
                dve.wait_ge(s.xc_ready, i + 1)
                v.tensor_tensor(SQ[:, :, :], XC[:, par, :, :], XC[:, par, :, :], ALU.mult).then_inc(s.sq_ready, 1)
                dve.wait_ge(s.sq_ready, i + 1)
                v.tensor_reduce(var[:, :], SQ[:, :, :], axis=AX, op=ALU.add).then_inc(s.sqsum_ready, 1)
                dve.wait_ge(s.sqsum_ready, i + 1)
                v.tensor_scalar(stat[:, par, 2, :], var[:, :], 1.0 / D, EPS, ALU.mult, ALU.add)\
                    .then_inc(s.var_ready, 1)

            def first_norms(s):
                norm_sum(s, 0, 0)
                for i in range(3):
                    norm_sum(s, i + 1, 1 - i % 2)
                    norm_squares(s, i, i % 2)

            def copy_v(s, i, par):
                if not known(i) or i >= 2:
                    dve.wait_ge(s.o_ps, i - 1)
                dve.wait_ge(s.xs_ready, i + 1)
                dve.wait_ge(consts_set, CONSTS)
                v.tensor_copy(V1[:, par, :, 0:D], XN[:, par, :, :]).then_inc(s.v_ready, 1)

            def copy_k(s, keys, made, i, par):
                dve.wait_ge(made, i + 1)
                if not known(i) or i >= 2:
                    dve.wait_ge(s.st_ps, i * 4 - 4)
                dve.wait_ge(consts_set, CONSTS)
                v.tensor_copy(K2[0:D, par, :], f32(keys[0:D, par, :])).then_inc(s.k2_ready, 1)

            def attention(s, base, layer):
                keys, made = (X2, s.x2_ready) if layer == 0 else (KS, s.kh_ready)

                def low_parts(i, par):
                    dve.wait_ge(s.qh_ready, i + 1)
                    if layer == 0:
                        v.tensor_tensor(Q2[0:D, par, :], bank[1][0:D, :], f32(QH[0:D, par, :]),
                                        ALU.subtract).then_inc(s.ql_ready, 1)
                        return
                    v.scalar_tensor_tensor(Q2[0:D, par, :], bank[1][0:D, :], w("bq", D), f32(QH[0:D, par, :]),
                                           ALU.add, ALU.subtract).then_inc(s.ql_ready, 1)
                    dve.wait_ge(s.kh_ready, i + 1)
                    a = at["bk"][0]
                    v.scalar_tensor_tensor(KS[D:P, par, :], bank[3][D:P, :], W[D:P, a:a + 1],
                                           f32(KS[D:P, par, :]), ALU.add, ALU.subtract).then_inc(s.kl_ready, 1)
                    dve.wait_ge(s.v_ps, i + 1)
                    o = bank[2][:, :].rearrange("p (t a d) -> p t a d", t=NT, a=2)
                    v.tensor_tensor(V1[:, par, :, 0:D], o[:, :, 0, :],
                                    VB[:, :].unsqueeze(1).to_broadcast([P, NT, D]), ALU.add).then_inc(s.vh_done, 1)
                    dve.wait_ge(s.vh_done, i + 1)
                    v.tensor_tensor(V1[:, par, :, 0:D], o[:, :, 1, :], V1[:, par, :, 0:D],
                                    ALU.add).then_inc(s.v_ready, 1)

                def maxima(i, par):
                    for t in range(NT):
                        dve.wait_ge(s.s_ps, i * NT + (t + 1))
                        v.tensor_reduce(nmax[:, par, t:t + 1], bank[2 + t % 2][:, :], axis=AX, op=ALU.max,
                                        negate=True).then_inc(s.max_ready, 1)

                def finish(i, par):
                    o = bank[7][:, :].rearrange("p (t d) -> p t d", t=NT)
                    dve.wait_ge(s.back_ps, i + 1)
                    c = base + i * 2
                    v.reciprocal(rec[:, :], o[:, :, D]).then_inc(dve_chain, 1)
                    dve.wait_ge(dve_chain, c + 1)
                    v.tensor_tensor(ON[:, :, :], o[:, :, 0:D], over(rec[:, :], D), ALU.mult).then_inc(dve_chain, 1)
                    dve.wait_ge(dve_chain, c + 2)
                    v.tensor_tensor(hb(i), hb(i), ON[:, :, :], ALU.add).then_inc(s.h_done, 1)

                norm_sum(s, 0, 0)
                norm_sum(s, 1, 1)
                norm_squares(s, 0, 0)
                norm_sum(s, 2, 0)
                norm_squares(s, 1, 1)
                norm_sum(s, 3, 1)
                low_parts(0, 0)
                if layer == 0:
                    copy_v(s, 0, 0)
                copy_k(s, keys, made, 0, 0)
                maxima(0, 0)
                norm_squares(s, 2, 0)

                def body(i, par):
                    if has(i + 4):
                        norm_sum(s, i + 4, par)
                    if layer == 0 and has(i + 1):
                        copy_v(s, i + 1, 1 - par)
                    if has(i + 3):
                        norm_squares(s, i + 3, 1 - par)
                    if has(i + 1):
                        low_parts(i + 1, 1 - par)
                        copy_k(s, keys, made, i + 1, 1 - par)
                    if not known(i) or i >= 1:
                        finish(i - 1, 1 - par)
                    if has(i + 1):
                        maxima(i + 1, 1 - par)

                sweep(dve, body)
                finish(NSEQ - 1, 1)

            dve.wait_ge(h0_ready, NSEQ)
            attention(a0, count[0], 0)
            dve.wait_ge(a0.h_done, NSEQ)

            base = count[0] + 2 * NSEQ

            def experts_of(i, par):
                if not known(i) or i >= 2:
                    dve.wait_ge(f0.l1_ps, i - 1)
                    dve.wait_ge(f0.h1_ready, i - 1)
                    dve.wait_ge(f0.h2_ready, i - 1)
                dve.wait_ge(routed_in[par], i * (8 * NG) + (16 - 8 * par) * NG)
                for g in range(NG):
                    ins = v.tensor_tensor(WC[:, par, g, :], WR[:, par, g, :], WS[:, :], ALU.add)
                ins.then_inc(f0.wc_ready, 1)

            def group(ap, g):
                return ap.rearrange("k (t g p) -> k g t p", t=NT, g=NG)[:, g, :, :]

            def layer1(i, par):
                dve.wait_ge(f0.l1_ps, i + 1)
                for g in range(NG):
                    ins = v.tensor_scalar(group(F2[:, par, :], g), group(bank[3][:, :], g),
                                          WC[:, par, g, WROW + HID:WROW + HID + 1], 0.0, ALU.add, ALU.max)
                ins.then_inc(f0.h2_ready, 1)

            def add_back(s, i):
                dve.wait_ge(s.back_ps, i + 1)
                v.tensor_tensor(hb(i), hb(i), bank[7][:, :].rearrange("p (t d) -> p t d", t=NT)[:, :, 0:D],
                                ALU.add).then_inc(s.h_done, 1)

            experts_of(0, 0)
            first_norms(f0)

            def ffn0(i, par):
                if has(i + 4):
                    norm_sum(f0, i + 4, par)
                if has(i + 3):
                    norm_squares(f0, i + 3, 1 - par)
                if not known(i) or i >= 3:
                    add_back(f0, i - 3)
                if not known(i) or i >= 1:
                    layer1(i - 1, 1 - par)
                if has(i + 1):
                    experts_of(i + 1, 1 - par)

            sweep(dve, ffn0)
            add_back(f0, NSEQ - 3)
            layer1(NSEQ - 1, 1)
            add_back(f0, NSEQ - 2)
            add_back(f0, NSEQ - 1)
            dve.wait_ge(f0.h_done, NSEQ)

            attention(a1, base, 1)
            dve.wait_ge(a1.h_done, NSEQ)

            GATE = 2 * NT + 4
            link_base = base + 2 * NSEQ
            v.memset(g16[:, :, :], NONE).then_inc(dve_chain, 1)
            dve.wait_ge(dve_chain, link_base + 1)
            base1 = link_base + 1

            def gate_sum(i):
                c = base1 + i * GATE
                dve.wait_ge(f1.g_ps, i + 1)
                o = bank[1][:, 0:NT * 2 * NEXP1].rearrange("p (t a e) -> p t a e", t=NT, a=2)
                v.tensor_tensor(gs[:, :, :], o[:, :, 0, :],
                                w("bg").unsqueeze(1).to_broadcast([P, NT, NEXP1]), ALU.add).then_inc(dve_chain, 1)
                dve.wait_ge(dve_chain, c + 1)
                v.tensor_tensor(g16[:, :, 0:NEXP1], o[:, :, 1, :], gs[:, :, :], ALU.add).then_inc(dve_chain, 1)

            def gate_sort(i, meanwhile):
                dve.wait_ge(dve_chain, base1 + i * GATE + 2)
                meanwhile()
                for t in range(NT):
                    v.max(top[:, t, :], g16[:, t, 0:NEXP1]).then_inc(dve_chain, 1)

            def gate_choose(i, meanwhile):
                c = base1 + i * GATE
                dve.wait_ge(dve_chain, c + 2 + NT)
                v.memset(top[:, :, TOPK:], NONE).then_inc(dve_chain, 1)
                dve.wait_ge(dve_chain, c + 3 + NT)
                meanwhile()
                for t in range(NT):
                    v.match_replace(took[:, t, :], top[:, t, :], g16[:, t, :], TAKEN).then_inc(dve_chain, 1)

            def gate_masks(i):
                c = base1 + i * GATE
                dve.wait_ge(dve_chain, c + 3 + 2 * NT)
                if not known(i) or i >= 1:
                    dve.wait_ge(f1.mt_ps, i)
                v.tensor_scalar(MK[:, :, D:D + NEXP1], took[:, :, 0:NEXP1], TAKEN / 2, -1.0,
                                ALU.is_lt, ALU.mult).then_inc(dve_chain, 1)
                v.tensor_scalar(MK[:, :, D + NEXP1:D + 2 * NEXP1], took[:, :, 0:NEXP1], TAKEN / 2, None,
                                ALU.is_gt).then_inc(f1.mk_ready, 1)

            def copy_xh(i, par):
                dve.wait_ge(f1.x2_ready, i + 1)
                if not known(i) or i >= 2:
                    dve.wait_ge(f1.b2_ps, i - 1)
                    dve.wait_ge(f1.u_ps, i * NEXP1 - NEXP1)
                v.tensor_copy(K2[0:D, par, :], f32(X2[0:D, par, :])).then_inc(f1.xh_ready, 1)

            def high(i, e):
                dve.wait_ge(f1.gelu_ready, i * NEXP1 + (e + 1))
                if not known(i) or i >= 1:
                    dve.wait_ge(f1.down_ps, i * NEXP1 + (e - 7))
                v.tensor_copy(GH[:, e, :], G[:, e, :]).then_inc(f1.high_ready, 1)

            def low(i, e):
                dve.wait_ge(f1.high_ready, i * NEXP1 + (e + 1))
                v.tensor_tensor(GL[:, e, :], G[:, e, :], f32(GH[:, e, :]), ALU.subtract).then_inc(f1.low_dve, 1)

            def add_halves(i):
                dve.wait_ge(f1.back_ps, i + 1)
                o = bank[7][:, :].rearrange("p (t d) -> p t d", t=NT)
                v.tensor_tensor(hb(i), hb(i), o[:, :, 0:D], ALU.add).then_inc(f1.h_half, 1)
                dve.wait_ge(f1.h_half, i + 1)
                v.tensor_tensor(hb(i), hb(i), o[:, :, D:2 * D], ALU.add).then_inc(f1.h_done, 1)

            first_norms(f1)
            copy_xh(0, 0)
            gate_sum(0)
            gate_sort(0, lambda: None)
            gate_choose(0, lambda: None)
            gate_masks(0)

            def ffn1(i, par):
                if has(i + 4):
                    norm_sum(f1, i + 4, par)
                if not known(i) or i >= 2:
                    add_halves(i - 2)
                high(i, 0)
                if has(i + 1):
                    gate_sum(i + 1)
                low(i, 0)
                if has(i + 1):
                    gate_sort(i + 1, lambda: high(i, 1))
                else:
                    high(i, 1)
                if has(i + 1):
                    gate_choose(i + 1, lambda: high(i, 2))
                else:
                    high(i, 2)
                low(i, 2)
                if has(i + 1):
                    gate_masks(i + 1)
                high(i, 3)
                if has(i + 1):
                    copy_xh(i + 1, 1 - par)
                high(i, 4)
                if has(i + 3):
                    norm_squares(f1, i + 3, 1 - par)
                low(i, 4)
                high(i, 5)
                high(i, 6)
                low(i, 6)
                high(i, 7)

            sweep(dve, ffn1)
            add_halves(NSEQ - 2)
            add_halves(NSEQ - 1)

        @block.tensor
        def _(pe):
            mm = nc.tensor.matmul

            pe.wait_ge(pack_in, 16)
            mm(bank[5][:, 0:P], w("wq0", D), w("wk0", D), start=True, stop=True)
            mm(bank[6][:, 0:D], w("wv", D), w("wo1", D), start=True, stop=True)
            mm(bank[7][:, 0:D], w("bvc", D + 1), w("wo1", D + 1), start=True, stop=True).then_inc(prod_ready, 1)

            pe.wait_ge(consts_set, CONSTS)
            def embed(i, par):
                pe.wait_ge(oh_ready, i + 1)
                pe.wait_ge(op_ready, i + 1)
                if not known(i) or i >= 2:
                    pe.wait_ge(h0_ready, i - 1)
                for t in range(NT):
                    o = bank[par][:, t * D:(t + 1) * D]
                    cols = slice(t * P, (t + 1) * P)
                    for k in range(3):
                        mm(o, OH[:, par, cols], T3[:, 0, k, :], start=(k == 0), stop=False)
                        last = mm(o, OP[:, par, cols], T3[0:NSEQ, 1, k, :], start=False, stop=(k == 2))
                last.then_inc(emb_ready, 1)

            sweep(pe, embed)

            def turn(s, i, par):
                pe.wait_ge(s.xs_ready, i + 1)
                for t in range(NT):
                    last = nc.tensor.transpose(bank[0][:, t * P:(t + 1) * P], f32(XS[:, par, t, :]), w("ident"))
                last.then_inc(s.xt_ready, 1)

            def turn_back(s, i, par):
                pe.wait_ge(s.ot_ready, i + 1)
                if not known(i) or i >= 1:
                    pe.wait_ge(s.h_done, i)
                for t in range(NT):
                    last = nc.tensor.transpose(bank[7][:, t * P:(t + 1) * P], OT[:, par, t * P:(t + 1) * P],
                                               w("ident"))
                last.then_inc(s.back_ps, 1)

            def attention(s, layer):
                keys = X2 if layer == 0 else KS

                def project(i, par):
                    pe.wait_ge(s.x2_ready, i + 1)
                    if not known(i) or i >= 1:
                        pe.wait_ge(s.ql_ready, i)
                    hi, lo = (AH[:, :], AL[:, :]) if layer == 0 else (wh("wq1"), wl("wq1"))
                    mm(bank[1][:, :], hi, X2[:, par, :], start=True, stop=False)
                    mm(bank[1][:, :], lo, X2[:, par, :], start=False, stop=True).then_inc(s.q_ps, 1)
                    if layer == 0:
                        return
                    if not known(i) or i >= 1:
                        pe.wait_ge(s.max_ready, i * NT)
                    mm(bank[3][:, :], wh("wk1"), X2[:, par, :], start=True, stop=False)
                    mm(bank[3][:, :], wl("wk1"), X2[:, par, :], start=False, stop=True).then_inc(s.k_ps, 1)
                    for t in range(NT):
                        last = mm(bank[2][:, t * P:(t + 1) * P], X2[:, par, t * P:(t + 1) * P], VHL[:, :],
                                  start=True, stop=True)
                    last.then_inc(s.v_ps, 1)

                def scores_for_max(i, par, t):
                    if t == 0:
                        pe.wait_ge(s.qh_ready, i + 1)
                        if layer == 1:
                            pe.wait_ge(s.kl_ready, i + 1)
                            pe.wait_ge(s.v_ready, i + 1)
                    if t >= 2:
                        pe.wait_ge(s.max_ready, i * NT + (t - 1))
                    elif not known(i) or i >= 1:
                        pe.wait_ge(s.max_ready, i * NT + (t - 1))
                    mm(bank[2 + t % 2][:, :], QH[:, par, t * P:(t + 1) * P], keys[:, par, :],
                       start=True, stop=True).then_inc(s.s_ps, 1)

                def spread_max(i, par):
                    pe.wait_ge(s.max_ready, i * NT + NT)
                    if not known(i) or i >= 1:
                        pe.wait_ge(s.m_ready, i)
                    if not known(i) or i >= 2:
                        pe.wait_ge(s.h_done, i - 1)
                    for t in range(NT):
                        last = mm(bank[7][:, t * P:(t + 1) * P], nmax[:, par, t:t + 1].to_broadcast([P, P]),
                                  IR[:, :], start=True, stop=True)
                    last.then_inc(s.m_ps, 1)

                def scores(i, par, kt):
                    if kt == 0:
                        pe.wait_ge(s.m_ready, i + 1)
                        pe.wait_ge(s.ql_ready, i + 1)
                        pe.wait_ge(s.k2_ready, i + 1)
                    if kt >= 2 or not known(i) or i >= 1:
                        pe.wait_ge(s.e_ready, i * NT + (kt - 1))
                    cols = slice(kt * P, (kt + 1) * P)
                    o = bank[4 + kt % 2][:, :]
                    mm(o, keys[:, par, cols], QH[:, par, :], start=True, stop=False)
                    mm(o, K2[0:D + 1, par, cols], Q2[0:D + 1, par, :], start=False, stop=True).then_inc(s.st_ps, 1)

                def values(i, par, kt):
                    pe.wait_ge(s.e_ready, i * NT + (kt + 1))
                    if kt == 0:
                        pe.wait_ge(s.v_ready, i + 1)
                        if not known(i) or i >= 1:
                            pe.wait_ge(s.ot_ready, i)
                    last = mm(bank[6][0:D + 1, :], V1[:, par, kt, :], PT[:, par, kt, :],
                              start=(kt == 0), stop=(kt == NT - 1))
                    if kt == NT - 1:
                        last.then_inc(s.o_ps, 1)

                turn(s, 0, 0)
                project(0, 0)
                turn(s, 1, 1)
                for t in range(NT):
                    scores_for_max(0, 0, t)

                def body(i, par):
                    spread_max(i, par)
                    if has(i + 1):
                        project(i + 1, 1 - par)
                    if has(i + 2):
                        turn(s, i + 2, par)
                    scores(i, par, 0)
                    scores(i, par, 1)
                    if not known(i) or i >= 1:
                        turn_back(s, i - 1, 1 - par)
                    scores(i, par, 2)
                    scores(i, par, 3)
                    if has(i + 1):
                        scores_for_max(i + 1, 1 - par, 0)
                        scores_for_max(i + 1, 1 - par, 1)
                    values(i, par, 0)
                    values(i, par, 1)
                    if has(i + 1):
                        scores_for_max(i + 1, 1 - par, 2)
                        scores_for_max(i + 1, 1 - par, 3)
                    values(i, par, 2)
                    values(i, par, 3)

                sweep(pe, body)
                turn_back(s, NSEQ - 1, 1)

            pe.wait_ge(prod_read, 1)
            pe.wait_ge(h0_ready, NSEQ)
            attention(a0, 0)
            pe.wait_ge(a0.h_done, NSEQ)

            def group(ap, g):
                return ap.rearrange("k (t g p) -> k g t p", t=NT, g=NG)[:, g, :, :]

            def enter0(i, par):
                pe.wait_ge(f0.x2_ready, i + 1)
                if not known(i) or i >= 1:
                    pe.wait_ge(f0.h0_ready, i)
                mm(bank[1][:, :], wh("wi"), X2[:, par, :], start=True, stop=False)
                mm(bank[1][:, :], wl("wi"), X2[:, par, :], start=False, stop=True).then_inc(f0.wi_ps, 1)

            def routed(i, par, l):
                src, dst, done = (F0, bank[2], f0.l0_ps) if l == 0 else (F1, bank[3], f0.l1_ps)
                if l == 0:
                    pe.wait_ge(f0.wc_ready, i + 1)
                    pe.wait_ge(f0.h0_ready, i + 1)
                    if not known(i) or i >= 1:
                        pe.wait_ge(f0.h1_ready, i)
                else:
                    pe.wait_ge(f0.h1_ready, i + 1)
                    if not known(i) or i >= 1:
                        pe.wait_ge(f0.h2_ready, i)
                for g in range(NG):
                    last = mm(group(dst[:, :], g), WC[:, par, g, l * WROW:l * WROW + HID],
                              group(src[:, par, :], g), start=True, stop=True)
                last.then_inc(done, 1)

            def leave0(i, par):
                pe.wait_ge(f0.h2_ready, i + 1)
                if not known(i) or i >= 1:
                    pe.wait_ge(f0.ot_ready, i)
                mm(bank[4][0:D, :], w("wo0"), F2[:, par, :], start=True, stop=True).then_inc(f0.o_ps, 1)

            turn(f0, 0, 0)
            enter0(0, 0)
            turn(f0, 1, 1)

            def ffn0(i, par):
                if has(i + 2):
                    pe.wait_ge(f0.x2_ready, i + 2)
                    turn(f0, i + 2, par)
                if has(i + 1):
                    enter0(i + 1, 1 - par)
                if not known(i) or i >= 2:
                    leave0(i - 2, par)
                if not known(i) or i >= 3:
                    turn_back(f0, i - 3, 1 - par)
                if not known(i) or i >= 1:
                    routed(i - 1, 1 - par, 1)
                routed(i, par, 0)

            sweep(pe, ffn0)
            turn_back(f0, NSEQ - 3, 1)
            leave0(NSEQ - 2, 0)
            routed(NSEQ - 1, 1, 1)
            turn_back(f0, NSEQ - 2, 0)
            leave0(NSEQ - 1, 1)
            turn_back(f0, NSEQ - 1, 1)
            pe.wait_ge(f0.h_done, NSEQ)

            attention(a1, 1)
            pe.wait_ge(a1.h_done, NSEQ)

            def gate_scores(i, par):
                pe.wait_ge(f1.x2_ready, i + 1)
                if not known(i) or i >= 1:
                    pe.wait_ge(f1.mk_ready, i)
                for t in range(NT):
                    last = mm(bank[1][:, t * 2 * NEXP1:(t + 1) * 2 * NEXP1], X2[:, par, t * P:(t + 1) * P],
                              GHL[:, :], start=True, stop=True)
                last.then_inc(f1.g_ps, 1)

            def turn_masks(i, par):
                pe.wait_ge(f1.mk_ready, i + 1)
                if not known(i) or i >= 1:
                    pe.wait_ge(f1.m2_ready, i)
                for t in range(NT):
                    last = nc.tensor.transpose(bank[2][:, t * P:(t + 1) * P], MK[:, t, :], w("ident"))
                last.then_inc(f1.mt_ps, 1)

            def up(i, par, e):
                if e == 0:
                    pe.wait_ge(f1.xh_ready, i + 1)
                    pe.wait_ge(f1.m2_ready, i + 1)
                if e >= 2:
                    pe.wait_ge(f1.gelu_ready, i * NEXP1 + (e - 1))
                elif not known(i) or i >= 1:
                    pe.wait_ge(f1.gelu_ready, i * NEXP1)
                a = at["w1"][0] + e * HID
                o = bank[3 + e % 2][:, :]
                mm(o, WH[:, a:a + HID], X2[:, par, :], start=True, stop=False)
                mm(o, WL[0:D + 2 * NEXP1, a:a + HID], K2[0:D + 2 * NEXP1, par, :], start=False, stop=True)\
                    .then_inc(f1.u_ps, 1)

            def down_bias(i, par):
                if not known(i) or i >= 2:
                    pe.wait_ge(f1.ot_ready, i - 1)
                rows = D + 2 * NEXP1
                mm(bank[5 + par][:, :], B2[0:rows, :], K2[0:rows, par, :], start=True, stop=False)\
                    .then_inc(f1.b2_ps, 1)

            def down(i, par, e):
                split = f1.low_dve if e % 2 == 0 else f1.low_pool
                pe.wait_ge(split, i * 4 + (e // 2 + 1))
                o = bank[5 + par][:, :]
                mm(o, W2[:, e, :], GH[:, e, :], start=False, stop=False)
                last = mm(o, W2[:, e, :], GL[:, e, :], start=False, stop=(e == NEXP1 - 1))
                last.then_inc(f1.down_ps, 1)

            turn(f1, 0, 0)
            gate_scores(0, 0)
            turn(f1, 1, 1)
            turn_masks(0, 0)

            def ffn1(i, par):
                for e in range(NEXP1):
                    up(i, par, e)
                    if e < LAG:
                        if not known(i) or i >= 1:
                            down(i - 1, 1 - par, e + NEXP1 - LAG)
                    else:
                        if e == LAG:
                            down_bias(i, par)
                        down(i, par, e - LAG)
                    if e == 0 and has(i + 1):
                        gate_scores(i + 1, 1 - par)
                    if e == 5 and has(i + 1):
                        turn_masks(i + 1, 1 - par)
                    if e == 7 and (not known(i) or i >= 1):
                        turn_back(f1, i - 1, 1 - par)
                if has(i + 2):
                    pe.wait_ge(f1.x2_ready, i + 2)
                    turn(f1, i + 2, par)

            sweep(pe, ffn1)
            for e in range(NEXP1 - LAG, NEXP1):
                down(NSEQ - 1, 1, e)
            turn_back(f1, NSEQ - 1, 1)


def kernel(**inputs):
    import concourse.bacc as bacc
    from concourse.bass_utils import run_bass_kernel_spmd

    x = {k: np.asarray(v) for k, v in inputs.items()}
    at, width = columns()
    pack = np.zeros((P, width), np.float32)

    def put(name, value, row=0):
        value = np.asarray(value)
        if value.ndim == 1:
            value = value[:, None]
        a = at[name][0]
        pack[row:row + value.shape[0], a:a + value.shape[1]] = value

    def twice(m):
        return np.concatenate([m, m], 0)

    def wide(m):
        return np.concatenate([m, m], 1)

    put("wq0", wide(x["L0_attn_Wq"]))
    put("wk0", wide(x["L0_attn_Wk"]))
    put("wq1", twice(wide(x["L1_attn_Wq"].T)))
    put("wk1", twice(wide(x["L1_attn_Wk"].T)))
    put("bq", twice(x["L1_attn_bq"][:, None]))
    put("bk", twice(x["L1_attn_bk"][:, None]))
    put("wv", wide(x["L1_attn_Wv"]))
    put("wo1", x["L1_attn_Wo"].T)
    put("wo1", x["L1_attn_bo"][None, :], D)
    put("bvc", np.broadcast_to(x["L1_attn_bv"][:, None], (D, P)))
    put("bvc", np.ones((1, P), np.float32), D)
    put("wi", twice(x["L0_ffn_Wi"].T))
    put("bi", x["L0_ffn_bi"])
    put("wo0", x["L0_ffn_Wo"].T)
    put("bo0", x["L0_ffn_bo"])
    put("w1", twice(x["L1_ffn_W1"].transpose(1, 0, 2).reshape(D, NEXP1 * HID)))
    put("b1", x["L1_ffn_b1"].T)
    put("w2", x["L1_ffn_W2"].transpose(1, 0, 2).reshape(HID, NEXP1 * D))
    put("b2", x["L1_ffn_b2"], D + NEXP1)
    put("wg", twice(x["L1_ffn_Wg"]))
    put("bg", np.broadcast_to(x["L1_ffn_bg"][None, :], (P, NEXP1)))
    put("tok", x["L0_tok_token_W"])
    put("pe", x["L0_tok_pe"][:NSEQ])
    ws = np.zeros((P, NLAY0, WROW), np.float32)
    ws[:, :, :HID] = x["L0_ffn_Ws"][:, 0].transpose(2, 0, 1)
    ws[:, :, HID] = x["L0_ffn_bs"][:, 0].T
    put("ws", ws.reshape(P, NLAY0 * WROW))
    experts = np.zeros((NEXP0, P, NLAY0, WROW), np.float32)
    experts[:, :, :, :HID] = x["L0_ffn_Wr"].transpose(1, 3, 0, 2)
    experts[:, :, :, HID] = x["L0_ffn_br"].transpose(1, 2, 0)
    put("ident", np.eye(P, dtype=np.float32))
    put("iota", np.arange(P, dtype=np.float32))
    put("steps", np.broadcast_to(np.repeat(np.arange(NSEQ, dtype=np.float32), NT), (P, NSEQ * NT)))
    sel = np.zeros((NEXP1, NEXP1, HID), np.float32)
    for k in range(NEXP1):
        sel[k, k] = -OFF
    put("sel", sel.reshape(NEXP1, -1), D)

    nc = bacc.Bacc("TRN2", target_bir_lowering=False, num_devices=1)
    arrays = {
        "tokens": np.ascontiguousarray(x["x"]),
        "route": np.ascontiguousarray(x["L0_ffn_route_id"].reshape(1, -1)),
        "pack": pack,
        "experts": experts.reshape(NEXP0, P, NLAY0 * WROW),
    }
    args = [nc.dram_tensor(n, a.shape, mybir.dt.from_np(a.dtype), kind="ExternalInput").ap()
            for n, a in arrays.items()]
    out = nc.dram_tensor("out", (NSEQ, SEQ, D), F32, kind="ExternalOutput").ap()
    pos = nc.dram_tensor("pos", (NSEQ, SEQ), F32, kind="Internal").ap()
    tower_kernel(nc, *args, out, pos)
    result = run_bass_kernel_spmd(nc, [arrays], core_ids=[0])
    return result.results[0]["out"]
```

```python
from contextlib import ExitStack

import numpy as np

import concourse.bass as bass
from concourse import mybir

F32 = mybir.dt.float32
F32R = mybir.dt.float32r
BF16 = mybir.dt.bfloat16
I32 = mybir.dt.int32
ALU = mybir.AluOpType
ACT = mybir.ActivationFunctionType
AX = mybir.AxisListType.X

P = 128
NSEQ, SEQ, D = 32, 512, 64
NT = SEQ // P
HID = 128
NEXP0, NLAY0 = 16, 2
NEXP1, TOPK = 8, 2
VOCAB = 128
SEP_ID, PAD_ID = 13, 1
EPS = 1e-5
LOAD, LOADS = 2, 4
HOTS = 4
LAG = 6
PARTS = 3
ROWS = PARTS * NSEQ
PIECES = 6
EARLY = 16
CONSTS = 6
HIGHS, LOWS = 6, 5
SCALE = D ** -0.5
GROUP = SEQ * NSEQ // 64
NG = SEQ // GROUP
WROW = HID + 1
NONE, TAKEN = -3e38, 3e38
OFF = -(2.0 ** 100)

SPLIT = [("wq1", P), ("wk1", P), ("wi", HID), ("w1", NEXP1 * HID)]
HEAD = [("tok", D), ("pe", D), ("iota", 1), ("row", 1)]
PLAIN = [("wg", NEXP1), ("b2", D), ("w2", NEXP1 * D),
         ("wq0", P), ("wk0", P), ("wv", P), ("wo1", D), ("bvc", P),
         ("wo0", D), ("b1", NEXP1), ("bi", 1), ("bq", 1), ("bk", 1),
         ("bo0", 1), ("bg", NEXP1), ("ident", P), ("ws", NLAY0 * WROW)]


def columns():
    at, n = {}, 0
    for name, width in SPLIT + HEAD + PLAIN:
        at[name] = (n, n + width)
        n += width
    return at, n


class NormSignals:

    def __init__(self, sem, tag):
        self.xh_done = sem(f"{tag}_xh_done")
        self.sqsum_ready = sem(f"{tag}_sqsum_ready")
        self.sum_ready = sem(f"{tag}_sum_ready")
        self.xc_ready = sem(f"{tag}_xc_ready")
        self.sq_ready = sem(f"{tag}_sq_ready")
        self.var_ready = sem(f"{tag}_var_ready")
        self.xs_ready = sem(f"{tag}_xs_ready")
        self.xt_ready = sem(f"{tag}_xt_ready")
        self.x2_ready = sem(f"{tag}_x2_ready")
        self.h_done = sem(f"{tag}_h_done")


class AttentionSignals(NormSignals):

    def __init__(self, sem, tag):
        super().__init__(sem, tag)
        self.k2_ready = sem(f"{tag}_k2_ready")
        self.v_ready = sem(f"{tag}_v_ready")
        self.q_ps = sem(f"{tag}_q_ps")
        self.qh_ready = sem(f"{tag}_qh_ready")
        self.ql_ready = sem(f"{tag}_ql_ready")
        self.s_ps = sem(f"{tag}_s_ps")
        self.max_ready = sem(f"{tag}_max_ready")
        self.m_ps = sem(f"{tag}_m_ps")
        self.m_ready = sem(f"{tag}_m_ready")
        self.st_ps = sem(f"{tag}_st_ps")
        self.e_ready = sem(f"{tag}_e_ready")
        self.o_ps = sem(f"{tag}_o_ps")
        self.ot_ready = sem(f"{tag}_ot_ready")
        self.back_ps = sem(f"{tag}_back_ps")
        self.k_ps = sem(f"{tag}_k_ps")
        self.kh_ready = sem(f"{tag}_kh_ready")
        self.kl_ready = sem(f"{tag}_kl_ready")
        self.v_ps = sem(f"{tag}_v_ps")
        self.vh_done = sem(f"{tag}_vh_done")


class RoutedSignals(NormSignals):

    def __init__(self, sem, tag):
        super().__init__(sem, tag)
        self.wc_ready = sem(f"{tag}_wc_ready")
        self.wi_ps = sem(f"{tag}_wi_ps")
        self.h0_ready = sem(f"{tag}_h0_ready")
        self.l0_ps = sem(f"{tag}_l0_ps")
        self.h1_ready = sem(f"{tag}_h1_ready")
        self.l1_ps = sem(f"{tag}_l1_ps")
        self.h2_ready = sem(f"{tag}_h2_ready")
        self.o_ps = sem(f"{tag}_o_ps")
        self.ot_ready = sem(f"{tag}_ot_ready")
        self.back_ps = sem(f"{tag}_back_ps")


class MixtureSignals(NormSignals):

    def __init__(self, sem, tag):
        super().__init__(sem, tag)
        self.xh_ready = sem(f"{tag}_xh_ready")
        self.g_ps = sem(f"{tag}_g_ps")
        self.mk_ready = sem(f"{tag}_mk_ready")
        self.b2_ps = sem(f"{tag}_b2_ps")
        self.mt_ps = sem(f"{tag}_mt_ps")
        self.m2_ready = sem(f"{tag}_m2_ready")
        self.u_ps = sem(f"{tag}_u_ps")
        self.gelu_ready = sem(f"{tag}_gelu_ready")
        self.high_ready = sem(f"{tag}_high_ready")
        self.low_dve = sem(f"{tag}_low_dve")
        self.low_pool = sem(f"{tag}_low_pool")
        self.down_ps = sem(f"{tag}_down_ps")
        self.h_half = sem(f"{tag}_h_half")
        self.ot_ready = sem(f"{tag}_ot_ready")
        self.back_ps = sem(f"{tag}_back_ps")


def sweep(eng, body, start=0, first=4, last=NSEQ - 6):
    for i in range(start, first):
        body(i, i % 2)
    with eng.Fori(first // 2, last // 2) as pair:
        body(pair * 2, 0)
        body(pair * 2 + 1, 1)
    for i in range(last, NSEQ):
        body(i, i % 2)


def known(i):
    return isinstance(i, int)


def has(i):
    return not known(i) or i < NSEQ


def tower_kernel(nc, tokens, route, pack, experts, out, ids_dram, pos_dram):
    at, width = columns()
    n_split = at[SPLIT[-1][0]][1]
    n_head = at[HEAD[-1][0]][1]

    with ExitStack() as ctx:
        def sb(name, shape, dt=F32):
            return ctx.enter_context(nc.sbuf_tensor(name, shape, dt))

        def ps(name):
            return ctx.enter_context(nc.psum_tensor(name, [P, 512], F32))

        def sem(name):
            return ctx.enter_context(nc.semaphore(name))

        H = sb("H", [P, NSEQ, NT, D])
        W = sb("W", [P, width])
        WH = sb("WH", [P, n_split], F32R)
        WL = sb("WL", [P, n_split], F32R)
        WR = sb("WR", [P, 2, NG, NLAY0 * WROW])
        WS = sb("WS", [P, NLAY0 * WROW])
        WC = sb("WC", [P, 2, NG, NLAY0 * WROW])
        AH = sb("AH", [P, P], F32R)
        AL = sb("AL", [P, P], F32R)
        VHL = sb("VHL", [P, 2 * D], F32R)
        B2 = sb("B2", [P, 2 * D], F32R)
        GHL = sb("GHL", [P, 2 * NEXP1], F32R)
        T3 = sb("T3", [P, 2, PARTS, D], BF16)
        TP = sb("TP", [ROWS, D], BF16)
        rest = sb("rest", [P, 2, D])
        VB = sb("VB", [P, D])
        IR = sb("IR", [P, P], F32R)
        IB = sb("IB", [P, P], BF16)
        half = sb("half", [P, NT])
        ninv = sb("ninv", [P, NT])
        route_sb = sb("route_sb", [1, NSEQ * NG], I32)

        tk = sb("tk", [P, NSEQ * NT], I32)
        sep = sb("sep", [P, NT * NSEQ])
        pad = sb("pad", [P, NT * NSEQ])
        carry = sb("carry", [P, NT * NSEQ])
        skip = sb("skip", [P, NT * NSEQ])
        kept = sb("kept", [P, NT * NSEQ])
        inner = sb("inner", [P, NT * NSEQ])
        run = sb("run", [P, NT * NSEQ])
        pos = sb("pos1", [P, NT * NSEQ])
        idn = sb("idn", [P, NSEQ * NT], BF16)
        posn = sb("posn", [P, NSEQ * NT], BF16)
        posb = sb("posb", [ROWS, LOADS, LOAD, SEQ], BF16)
        OH = sb("OH", [P, HOTS, SEQ], BF16)
        OP = sb("OP", [ROWS, HOTS, SEQ], BF16)

        stat = sb("stat", [P, 2, 4, NT])
        var = sb("var", [P, NT])
        XC = sb("XC", [P, 2, NT, D])
        SQ = sb("SQ", [P, NT, D])
        XN = sb("XN", [P, 2, NT, D])
        XS = sb("XS", [P, 2, NT, 2 * D], F32R)
        X2 = sb("X2", [P, 2, SEQ], F32R)
        KS = sb("KS", [P, 2, SEQ], F32R)
        K2 = sb("K2", [P, 2, SEQ], F32R)
        QH = sb("QH", [P, 2, SEQ], F32R)
        Q2 = sb("Q2", [P, 2, SEQ], F32R)
        V1 = sb("V1", [P, 2, NT, D + 1])
        PT = sb("PT", [P, 2, NT, SEQ])
        nmax = sb("nmax", [P, 2, NT], F32R)
        rec = sb("rec", [P, NT])
        ON = sb("ON", [P, NT, D])
        OT = sb("OT", [P, 2, SEQ])
        F0 = sb("F0", [P, 2, SEQ])
        F1 = sb("F1", [P, 2, SEQ])
        F2 = sb("F2", [P, 2, SEQ])
        idb = PT[:, :, :, :].bitcast(BF16).rearrange("p a t n -> p (a t n)")\
            .rearrange("p (l s n) -> p l s n", l=LOADS, n=SEQ)[:, :, 0:LOAD, :]
        G = PT[:, :, :, :].rearrange("p a t n -> p (a t) n")
        GH = sb("GH", [P, NEXP1, SEQ], F32R)
        GL = sb("GL", [P, NEXP1, SEQ], F32R)
        W2 = sb("W2", [P, NEXP1, 2 * D], F32R)
        gs = sb("gs", [P, NT, NEXP1])
        g16 = sb("g16", [P, NT, 2 * NEXP1])
        top = sb("top", [P, NT, NEXP1])
        took = sb("took", [P, NT, 2 * NEXP1])
        MK = sb("MK", [P, NT, P], BF16)

        bank = [ps(f"bank{k}") for k in range(8)]

        def w(name, rows=P):
            a, b = at[name]
            return W[0:rows, a:b]

        def wh(name, rows=P):
            a, b = at[name]
            return WH[0:rows, a:b]

        def wl(name, rows=P):
            a, b = at[name]
            return WL[0:rows, a:b]

        def f32(ap):
            return ap.bitcast(F32)

        def hb(i):
            return H[:, bass.ds(i, 1), :, :].rearrange("p a t d -> p (a t) d")

        def over(ap, n):
            return ap.unsqueeze(2).to_broadcast([P, NT, n])

        tok_in, head_in, pack_in, route_in = sem("tok_in"), sem("head_in"), sem("pack_in"), sem("route_in")
        high_set, low_set = sem("high_set"), sem("low_set")
        routed_in = [sem("routed_in0"), sem("routed_in1")]
        ids_out, pos_out, ids_in, pos_in, stored = (
            sem("ids_out"), sem("pos_out"), [sem(f"ids_in{k}") for k in range(LOADS)], [sem(f"pos_in{k}") for k in range(LOADS)], sem("stored"))
        dve_chain, gate_chain = sem("dve_chain"), sem("gate_chain")
        mean_done, sigma_done, xn_done = sem("mean_done"), sem("sigma_done"), sem("xn_done")
        consts_set, ids_ready, pos_ready, parts_ready, prod_ready, prod_read = (
            sem("consts_set"), sem("ids_ready"), sem("pos_ready"), sem("parts_ready"), sem("prod_ready"), sem("prod_read"))
        oh_ready, op_ready, emb_ready, h0_ready = sem("oh_ready"), sem("op_ready"), sem("emb_ready"), sem("h0_ready")

        a0, a1 = AttentionSignals(sem, "a0"), AttentionSignals(sem, "a1")
        f0, f1 = RoutedSignals(sem, "f0"), MixtureSignals(sem, "f1")

        block = ctx.enter_context(nc.Block())

        @block.sync
        def _(sp):
            sp.dma_start(tk[:, :].rearrange("p (s t) -> p s t", t=NT),
                         tokens.rearrange("s (p t) -> p s t", t=NT)).then_inc(tok_in, 16)
            sp.dma_start(W[:, n_split:n_head], pack[:, n_split:n_head]).then_inc(head_in, 16)
            sp.wait_ge(ids_ready, 1)
            sp.dma_start(ids_dram.rearrange("s (p t) -> p s t", t=NT),
                         idn[:, :].rearrange("p (s t) -> p s t", t=NT)).then_inc(ids_out, 16)
            sp.wait_ge(pos_ready, 1)
            sp.dma_start(pos_dram.rearrange("s (p t) -> p s t", t=NT),
                         posn[:, :].rearrange("p (s t) -> p s t", t=NT)).then_inc(pos_out, 16)
            sp.wait_ge(ids_out, 16)
            sp.wait_ge(pos_out, 16)

            def load_ids(k):
                slot = k % LOADS
                if k >= LOADS:
                    sp.wait_ge(op_ready, (k - LOADS + 1) * LOAD)
                rows = slice(k * LOAD, (k + 1) * LOAD)
                sp.dma_start(idb[:, slot, :, :],
                             ids_dram[rows, :].unsqueeze(0).to_broadcast([P, LOAD, SEQ])).then_inc(ids_in[slot], 16)
                sp.dma_start(posb[:, slot, :, :],
                             pos_dram[rows, :].unsqueeze(0).to_broadcast([ROWS, LOAD, SEQ])).then_inc(pos_in[slot], 16)

            step = -(-(width - n_head) // (PIECES - 2))
            pieces = [(a, min(a + step, width)) for a in range(n_head, width, step)]
            pieces += [(0, n_split // 2), (n_split // 2, n_split)]
            for k in range(NSEQ // LOAD):
                load_ids(k)
                if LOADS <= k + 1 < LOADS + PIECES:
                    a, b = pieces[k + 1 - LOADS]
                    sp.dma_start(W[:, a:b], pack[:, a:b]).then_inc(pack_in, 16)
            sp.dma_start(route_sb[:, :], route).then_inc(route_in, 16)

            def load_experts(i, par):
                if not known(i) or i >= 2:
                    sp.wait_ge(f0.wc_ready, i - 1)
                for g in range(NG):
                    expert = sp.value_load(route_sb[0:1, bass.ds(i * NG + g, 1)], min_val=0, max_val=NEXP0 - 1)
                    sp.dma_start(WR[:, par, g, :],
                                 experts[bass.ds(expert, 1), :, :].rearrange("a p n -> p (a n)"))\
                        .then_inc(routed_in[par], 16)

            sp.wait_ge(route_in, 16)
            sweep(sp, load_experts)
            out_rows = out.rearrange("b (p t) d -> p b (t d)", t=NT)

            def store(i, par):
                sp.wait_ge(f1.h_done, i + 1)
                sp.dma_start(out_rows[:, bass.ds(i, 1), :],
                             H[:, bass.ds(i, 1), :, :].rearrange("p a t d -> p a (t d)")).then_inc(stored, 16)

            sweep(sp, store)
            sp.wait_ge(stored, 16 * NSEQ)

        @block.gpsimd
        def _(pool):
            pl = nc.gpsimd

            pl.memset(half[:, :], -0.5).then_inc(consts_set, 1)
            pl.memset(ninv[:, :], -1.0 / D).then_inc(consts_set, 1)
            pl.memset(V1[:, :, :, :], 1.0).then_inc(consts_set, 1)
            pl.memset(f32(K2[:, :, :]), 1.0).then_inc(consts_set, 1)
            pl.memset(MK[:, :, :], 0.0).then_inc(consts_set, 1)
            pl.memset(OT[:, :, :], 0.0).then_inc(consts_set, 1)

            pool.wait_ge(consts_set, CONSTS)

            def norm_centre(s, before, phase, i, par):
                pool.wait_ge(s.sum_ready, i + 1)
                pl.tensor_tensor(stat[:, par, 1, :], stat[:, par, 0, :], ninv[:, :], ALU.mult).then_inc(mean_done, 1)
                pool.wait_ge(mean_done, phase * NSEQ + i + 1)
                if not known(i) or i >= 2:
                    pool.wait_ge(s.var_ready, i - 1)
                elif before is not None:
                    pool.wait_ge(before.var_ready, NSEQ - 1 + i)
                pl.tensor_tensor(XC[:, par, :, :], hb(i), over(stat[:, par, 1, :], D), ALU.add)\
                    .then_inc(s.xc_ready, 1)

            def norm_scale(s, before, phase, i, par):
                pool.wait_ge(s.var_ready, i + 1)
                pl.tensor_tensor(stat[:, par, 3, :], stat[:, par, 2, :], half[:, :], ALU.pow).then_inc(sigma_done, 1)
                pool.wait_ge(sigma_done, phase * NSEQ + i + 1)
                if s is a0 and (not known(i) or i >= 2):
                    pool.wait_ge(a0.v_ready, i - 1)
                elif before is a0 and known(i) and i < 2:
                    pool.wait_ge(a0.v_ready, NSEQ - 1 + i)
                scale = over(stat[:, par, 3, :], D)
                pl.tensor_tensor(XN[:, par, :, :], XC[:, par, :, :], scale, ALU.mult).then_inc(xn_done, 1)
                if not known(i) or i >= 2:
                    pool.wait_ge(s.xt_ready, i - 1)
                elif before is not None:
                    pool.wait_ge(before.xt_ready, NSEQ - 1 + i)
                pl.tensor_tensor(XS[:, par, :, 0:D], XC[:, par, :, :], scale, ALU.mult).then_inc(s.xh_done, 1)
                pool.wait_ge(xn_done, phase * NSEQ + i + 1)
                pool.wait_ge(s.xh_done, i + 1)
                pl.tensor_tensor(XS[:, par, :, D:2 * D], XN[:, par, :, :], f32(XS[:, par, :, 0:D]),
                                 ALU.subtract).then_inc(s.xs_ready, 1)

            def centre_on(s, before, after, phase, i, par):
                if has(i):
                    norm_centre(s, before, phase, i, par)
                elif after is not None:
                    norm_centre(after, s, phase + 1, i - NSEQ, par)

            def scale_on(s, before, after, phase, i, par):
                if has(i):
                    norm_scale(s, before, phase, i, par)
                elif after is not None:
                    norm_scale(after, s, phase + 1, i - NSEQ, par)

            def norms(s, before, after, phase):
                def body(i, par):
                    centre_on(s, before, after, phase, i + 4, par)
                    scale_on(s, before, after, phase, i + 3, 1 - par)

                sweep(pool, body)

            pool.wait_ge(high_set, HIGHS)
            a, b = at["w1"]
            lows = [(WL[:, 0:a], W[:, 0:a], WH[:, 0:a]),
                    (WL[0:D, a:b], W[0:D, a:b], WH[0:D, a:b]),
                    (W2[:, :, D:2 * D], w("w2").rearrange("p (e d) -> p e d", e=NEXP1), W2[:, :, 0:D]),
                    (B2[:, D:2 * D], w("b2"), B2[:, 0:D]),
                    (GHL[:, NEXP1:2 * NEXP1], w("wg"), GHL[:, 0:NEXP1])]
            for low, full, high in lows:
                pl.tensor_tensor(low, full, f32(high), ALU.subtract).then_inc(low_set, 1)

            norm_centre(a0, None, 0, 0, 0)
            for i in range(3):
                norm_centre(a0, None, 0, i + 1, 1 - i % 2)
                norm_scale(a0, None, 0, i, i % 2)
            norms(a0, None, f0, 0)
            norms(f0, a0, a1, 1)
            norms(a1, f0, f1, 2)

            def low(i, e):
                pool.wait_ge(f1.high_ready, i * NEXP1 + (e + 1))
                pl.tensor_tensor(GL[:, e, :], G[:, e, :], f32(GH[:, e, :]), ALU.subtract).then_inc(f1.low_pool, 1)

            def ffn1(i, par):
                centre_on(f1, a1, None, 3, i + 4, par)
                low(i, 1)
                low(i, 3)
                low(i, 5)
                low(i, 7)
                scale_on(f1, a1, None, 3, i + 3, 1 - par)

            sweep(pool, ffn1)

        @block.scalar
        def _(act):
            sc_ = nc.scalar

            def embed(i, par):
                act.wait_ge(emb_ready, i + 1)
                sc_.activation(hb(i), bank[par][:, 0:NT * D].rearrange("p (t d) -> p t d", t=NT),
                               ACT.Copy).then_inc(h0_ready, 1)

            for i in range(EARLY):
                embed(i, i % 2)
            act.wait_ge(pack_in, 16 * PIECES)
            a, b = at["w1"]
            highs = [(WH[:, :], W[:, 0:n_split]),
                     (W2[:, :, 0:D], w("w2").rearrange("p (e d) -> p e d", e=NEXP1)),
                     (B2[:, 0:D], w("b2")),
                     (GHL[:, 0:NEXP1], w("wg")),
                     (IR[:, :], w("ident")),
                     (IB[:, :], w("ident"))]
            for k, (high, full) in enumerate(highs):
                embed(EARLY + k, k % 2)
                sc_.activation(high, full, ACT.Copy).then_inc(high_set, 1)
            for i in range(EARLY + HIGHS, EARLY + HIGHS + 2):
                embed(i, i % 2)
            sc_.activation(WL[D:P, a:b].rearrange("p (e n) -> p e n", e=NEXP1),
                           w("ident")[D:P, D:D + NEXP1].unsqueeze(2).to_broadcast([P - D, NEXP1, HID]),
                           ACT.Copy, scale=-OFF).then_inc(high_set, 1)
            sweep(act, embed, start=EARLY + HIGHS + 2, first=EARLY + HIGHS + 2)

            def evac_x(s, i, par):
                act.wait_ge(s.xt_ready, i + 1)
                if s is a0 and (not known(i) or i >= 2):
                    act.wait_ge(s.st_ps, i * NT - 4)
                elif s is f0 and known(i) and i < 2:
                    act.wait_ge(a0.st_ps, (NSEQ - 1 + i) * NT)
                sc_.activation(X2[:, par, :], bank[0][:, :], ACT.Copy).then_inc(s.x2_ready, 1)

            def evac_x_on(s, after, i, par):
                if has(i):
                    evac_x(s, i, par)
                else:
                    evac_x(after, i - NSEQ, par)

            def evac_o(s, before, src, rows, i, par):
                if s is f1:
                    act.wait_ge(s.down_ps, i * NEXP1 + NEXP1)
                else:
                    act.wait_ge(s.o_ps, i + 1)
                if not known(i) or i >= 2:
                    act.wait_ge(s.back_ps, i - 1)
                elif before is not None:
                    act.wait_ge(before.back_ps, NSEQ - 1 + i)
                if s is f0:
                    ins = sc_.activation(OT[0:rows, par, :], src[0:rows, :], ACT.Identity, bias=w("bo0", D))
                else:
                    ins = sc_.activation(OT[0:rows, par, :], src[0:rows, :], ACT.Copy)
                ins.then_inc(s.ot_ready, 1)

            def attention(s, before, after, layer, meanwhile):
                def evac_q(i, par):
                    act.wait_ge(s.q_ps, i + 1)
                    if layer == 0:
                        sc_.activation(QH[:, par, :], bank[1][:, :], ACT.Copy).then_inc(s.qh_ready, 1)
                    else:
                        sc_.activation(QH[:, par, :], bank[1][:, :], ACT.Identity,
                                       bias=w("bq")).then_inc(s.qh_ready, 1)
                        act.wait_ge(s.k_ps, i + 1)
                        sc_.activation(KS[:, par, :], bank[3][:, :], ACT.Identity,
                                       bias=w("bk")).then_inc(s.kh_ready, 1)

                if before is None:
                    evac_x(s, 0, 0)
                evac_q(0, 0)
                if before is None:
                    evac_x(s, 1, 1)

                def body(i, par):
                    if not known(i) or i >= 1:
                        evac_o(s, before, bank[6], D + 1, i - 1, 1 - par)
                    act.wait_ge(s.m_ps, i + 1)
                    sc_.activation(Q2[D:D + 1, par, :], bank[7][D:D + 1, :], ACT.Copy).then_inc(s.m_ready, 1)
                    if has(i + 1):
                        evac_q(i + 1, 1 - par)
                    for kt in range(NT):
                        act.wait_ge(s.st_ps, i * NT + (kt + 1))
                        if kt == 0 and (not known(i) or i >= 2):
                            act.wait_ge(s.o_ps, i - 1)
                        sc_.activation(PT[:, par, kt, :], bank[4 + kt % 2][:, :], ACT.Exp,
                                       scale=SCALE).then_inc(s.e_ready, 1)
                    evac_x_on(s, after, i + 2, par)

                sweep(act, body)
                meanwhile()
                evac_o(s, before, bank[6], D + 1, NSEQ - 1, 1)

            def ffn0_in(i, par):
                act.wait_ge(f0.wi_ps, i + 1)
                sc_.activation(F0[:, par, :], bank[1][:, :], ACT.Relu, bias=w("bi")).then_inc(f0.h0_ready, 1)

            attention(a0, None, f0, 0, lambda: ffn0_in(0, 0))

            def ffn0(i, par):
                evac_x_on(f0, a1, i + 2, par)
                if has(i + 1):
                    ffn0_in(i + 1, 1 - par)
                if not known(i) or i >= 2:
                    evac_o(f0, a0, bank[4], D, i - 2, par)
                act.wait_ge(f0.l0_ps, i + 1)
                act.wait_ge(f0.wc_ready, i + 1)
                for g in range(NG):
                    ins = sc_.activation(group(F1[:, par, :], g), group(bank[2][:, :], g), ACT.Relu,
                                         bias=WC[:, par, g, HID:HID + 1])
                ins.then_inc(f0.h1_ready, 1)

            def group(ap, g):
                return ap.rearrange("k (t g p) -> k g t p", t=NT, g=NG)[:, g, :, :]

            sweep(act, ffn0)
            evac_o(f0, a0, bank[4], D, NSEQ - 2, 0)
            evac_o(f0, a0, bank[4], D, NSEQ - 1, 1)
            attention(a1, f0, f1, 1, lambda: None)

            def masks(i, par):
                act.wait_ge(f1.mt_ps, i + 1)
                if not known(i) or i >= 2:
                    act.wait_ge(f1.b2_ps, i - 1)
                sc_.activation(K2[D:D + 2 * NEXP1, par, :], bank[2][D:D + 2 * NEXP1, :],
                               ACT.Copy).then_inc(f1.m2_ready, 1)

            masks(0, 0)

            def gelu(i, e):
                act.wait_ge(f1.u_ps, i * NEXP1 + (e + 1))
                if not known(i) or i >= 1:
                    split = f1.low_dve if e % 2 == 0 else f1.low_pool
                    act.wait_ge(split, i * 4 + (e // 2 - 3))
                sc_.activation(G[:, e, :], bank[3 + e % 2][:, :], ACT.Gelu,
                               bias=W[:, at["b1"][0] + e:at["b1"][0] + e + 1]).then_inc(f1.gelu_ready, 1)

            def ffn1(i, par):
                for e in range(5):
                    gelu(i, e)
                gelu(i, 5)
                if has(i + 1):
                    masks(i + 1, 1 - par)
                if not known(i) or i >= 1:
                    evac_o(f1, a1, bank[6 - par], P, i - 1, 1 - par)
                gelu(i, 6)
                gelu(i, 7)
                if has(i + 2):
                    evac_x(f1, i + 2, par)

            sweep(act, ffn1)
            evac_o(f1, a1, bank[6], P, NSEQ - 1, 1)

        @block.vector
        def _(dve):
            v = nc.vector
            count = [0]

            def link(ins):
                count[0] += 1
                ins.then_inc(dve_chain, 1)
                dve.wait_ge(dve_chain, count[0])

            def by_step(ap):
                return ap.rearrange("p (t s) -> p s t", t=NT)

            ids = tk[:, :].rearrange("p (s t) -> p s t", t=NT)
            v.memset(inner[:, :], 1.0)
            v.memset(skip[:, 0:1], 0.0)
            v.memset(by_step(pad[:, :])[:, 0:1, :], 0.0).then_inc(dve_chain, 1)
            count[0] += 1
            dve.wait_ge(dve_chain, count[0])
            link(v.memset(by_step(inner[:, :])[:, 0:1, :], 0.0))
            dve.wait_ge(tok_in, 16)
            v.tensor_copy(idn[:, :], tk[:, :]).then_inc(ids_ready, 1)
            v.tensor_scalar(by_step(sep[:, :]), ids, float(SEP_ID), None, ALU.is_equal)
            link(v.tensor_scalar(by_step(pad[:, :])[:, 1:, :], ids[:, 1:, :], float(PAD_ID), None, ALU.is_equal))
            link(v.tensor_tensor_scan(carry[:, :], pad[:, :], sep[:, :], 0.0, ALU.mult, ALU.max))
            link(v.tensor_tensor(skip[:, 1:], pad[:, 1:], carry[:, :-1], ALU.mult))
            link(v.tensor_scalar(kept[:, :], skip[:, :], -1.0, 1.0, ALU.mult, ALU.add))
            link(v.tensor_tensor_scan(run[:, :], inner[:, :], kept[:, :], 0.0, ALU.mult, ALU.add))
            link(v.scalar_tensor_tensor(pos[:, :], skip[:, :], -2.0 * NSEQ, run[:, :], ALU.mult, ALU.add))
            v.tensor_scalar(posn[:, :].rearrange("p (s t) -> p s t", t=NT), by_step(pos[:, :]), -1.0, None,
                            ALU.add).then_inc(pos_ready, 1)

            dve.wait_ge(head_in, 16)
            link(v.memset(w("tok", 1), 0.0))
            a = at["tok"][0]
            tables = W[:, a:a + 2 * D].rearrange("p (a d) -> p a d", a=2)
            link(v.tensor_copy(T3[:, :, 0, :], tables))
            link(v.tensor_tensor(rest[:, :, :], tables, T3[:, :, 0, :], ALU.subtract))
            link(v.tensor_copy(T3[:, :, 1, :], rest[:, :, :]))
            link(v.tensor_tensor(T3[:, :, 2, :], rest[:, :, :], T3[:, :, 1, :], ALU.subtract))
            for k in range(PARTS):
                rows = slice(k * NSEQ, (k + 1) * NSEQ)
                v.tensor_copy(TP[rows, :], T3[rows, 1, k, :]).then_inc(parts_ready, 1)

            def one_hots(i):
                k = i // LOAD
                at_ = k % LOADS, i % LOAD
                if i % LOAD == 0:
                    dve.wait_ge(ids_in[at_[0]], 16 * (k // LOADS + 1))
                    dve.wait_ge(pos_in[at_[0]], 16 * (k // LOADS + 1))
                if i >= HOTS:
                    dve.wait_ge(emb_ready, i - HOTS + 1)
                v.tensor_scalar(OH[:, i % HOTS, :].rearrange("k (t p) -> k t p", t=NT),
                                idb[:, at_[0], at_[1], :].rearrange("k (p t) -> k t p", t=NT),
                                w("iota"), None, ALU.is_equal).then_inc(oh_ready, 1)
                v.tensor_scalar(OP[:, i % HOTS, :].rearrange("k (t p) -> k t p", t=NT),
                                posb[:, at_[0], at_[1], :].rearrange("k (p t) -> k t p", t=NT),
                                w("row", ROWS), None, ALU.is_equal).then_inc(op_ready, 1)

            def norm_sum(s, i, par):
                v.tensor_reduce(stat[:, par, 0, :], hb(i), axis=AX, op=ALU.add).then_inc(s.sum_ready, 1)

            def norm_squares(s, i, par):
                dve.wait_ge(s.xc_ready, i + 1)
                v.tensor_tensor(SQ[:, :, :], XC[:, par, :, :], XC[:, par, :, :], ALU.mult).then_inc(s.sq_ready, 1)
                dve.wait_ge(s.sq_ready, i + 1)
                v.tensor_reduce(var[:, :], SQ[:, :, :], axis=AX, op=ALU.add).then_inc(s.sqsum_ready, 1)
                dve.wait_ge(s.sqsum_ready, i + 1)
                v.tensor_scalar(stat[:, par, 2, :], var[:, :], 1.0 / D, EPS, ALU.mult, ALU.add)\
                    .then_inc(s.var_ready, 1)

            def first_norms(s, i):
                par = i % 2
                dve.wait_ge(h0_ready, i + 1)
                norm_sum(s, i, par)
                if i >= 1:
                    norm_squares(s, i - 1, 1 - par)
                if i == 3:
                    norm_sum(s, 4, 0)
                    norm_squares(s, 3, 1)

            def products():
                dve.wait_ge(prod_ready, 1)
                v.tensor_copy(VB[:, :], bank[7][:, 0:D])
                v.tensor_copy(VHL[:, 0:D], bank[6][:, 0:D])
                v.tensor_copy(WS[:, :], w("ws"))
                link(v.tensor_copy(AH[:, :], bank[5][:, 0:P]))
                for l in range(NLAY0):
                    v.tensor_tensor(WS[:, l * WROW:l * WROW + HID], WS[:, l * WROW:l * WROW + HID],
                                    w("ident"), ALU.add)
                v.tensor_tensor(VHL[:, D:2 * D], bank[6][:, 0:D], f32(VHL[:, 0:D]), ALU.subtract)
                v.tensor_tensor(AL[:, :], bank[5][:, 0:P], f32(AH[:, :]), ALU.subtract).then_inc(prod_read, 1)

            for i in range(NSEQ):
                one_hots(i)
                if i == EARLY + 4:
                    products()
                if i >= NSEQ - 4:
                    first_norms(a0, i - (NSEQ - 4))

            def sum_on(s, after, i, par):
                if has(i):
                    norm_sum(s, i, par)
                elif after is not None:
                    dve.wait_ge(s.h_done, i - NSEQ + 1)
                    norm_sum(after, i - NSEQ, par)

            def squares_on(s, after, i, par):
                if has(i):
                    norm_squares(s, i, par)
                elif after is not None:
                    norm_squares(after, i - NSEQ, par)

            def copy_v(s, i, par):
                if not known(i) or i >= 2:
                    dve.wait_ge(s.o_ps, i - 1)
                dve.wait_ge(s.xs_ready, i + 1)
                dve.wait_ge(consts_set, CONSTS)
                v.tensor_copy(V1[:, par, :, 0:D], XN[:, par, :, :]).then_inc(s.v_ready, 1)

            def copy_k(s, keys, made, i, par):
                dve.wait_ge(made, i + 1)
                if not known(i) or i >= 2:
                    dve.wait_ge(s.st_ps, i * 4 - 4)
                dve.wait_ge(consts_set, CONSTS)
                v.tensor_copy(K2[0:D, par, :], f32(keys[0:D, par, :])).then_inc(s.k2_ready, 1)

            def attention(s, after, base, layer, meanwhile):
                keys, made = (X2, s.x2_ready) if layer == 0 else (KS, s.kh_ready)

                def low_parts(i, par):
                    dve.wait_ge(s.qh_ready, i + 1)
                    if layer == 0:
                        v.tensor_tensor(Q2[0:D, par, :], bank[1][0:D, :], f32(QH[0:D, par, :]),
                                        ALU.subtract).then_inc(s.ql_ready, 1)
                        return
                    v.scalar_tensor_tensor(Q2[0:D, par, :], bank[1][0:D, :], w("bq", D), f32(QH[0:D, par, :]),
                                           ALU.add, ALU.subtract).then_inc(s.ql_ready, 1)
                    dve.wait_ge(s.kh_ready, i + 1)
                    a = at["bk"][0]
                    v.scalar_tensor_tensor(KS[D:P, par, :], bank[3][D:P, :], W[D:P, a:a + 1],
                                           f32(KS[D:P, par, :]), ALU.add, ALU.subtract).then_inc(s.kl_ready, 1)
                    dve.wait_ge(s.v_ps, i + 1)
                    o = bank[2][:, :].rearrange("p (t a d) -> p t a d", t=NT, a=2)
                    v.tensor_tensor(V1[:, par, :, 0:D], o[:, :, 0, :],
                                    VB[:, :].unsqueeze(1).to_broadcast([P, NT, D]), ALU.add).then_inc(s.vh_done, 1)
                    dve.wait_ge(s.vh_done, i + 1)
                    v.tensor_tensor(V1[:, par, :, 0:D], o[:, :, 1, :], V1[:, par, :, 0:D],
                                    ALU.add).then_inc(s.v_ready, 1)

                def maxima(i, par):
                    for t in range(NT):
                        dve.wait_ge(s.s_ps, i * NT + (t + 1))
                        v.tensor_reduce(nmax[:, par, t:t + 1], bank[2 + t % 2][:, :], axis=AX, op=ALU.max,
                                        negate=True).then_inc(s.max_ready, 1)

                def finish(i, par):
                    o = bank[7][:, :].rearrange("p (t d) -> p t d", t=NT)
                    dve.wait_ge(s.back_ps, i + 1)
                    c = base + i * 2
                    v.reciprocal(rec[:, :], o[:, :, D]).then_inc(dve_chain, 1)
                    dve.wait_ge(dve_chain, c + 1)
                    v.tensor_tensor(ON[:, :, :], o[:, :, 0:D], over(rec[:, :], D), ALU.mult).then_inc(dve_chain, 1)
                    dve.wait_ge(dve_chain, c + 2)
                    v.tensor_tensor(hb(i), hb(i), ON[:, :, :], ALU.add).then_inc(s.h_done, 1)

                if layer == 0:
                    copy_v(s, 0, 0)
                low_parts(0, 0)
                copy_k(s, keys, made, 0, 0)
                maxima(0, 0)

                def body(i, par):
                    if layer == 0 and has(i + 1):
                        copy_v(s, i + 1, 1 - par)
                    squares_on(s, after, i + 4, par)
                    sum_on(s, after, i + 5, 1 - par)
                    if has(i + 1):
                        low_parts(i + 1, 1 - par)
                        copy_k(s, keys, made, i + 1, 1 - par)
                    if not known(i) or i >= 1:
                        finish(i - 1, 1 - par)
                    if has(i + 1):
                        maxima(i + 1, 1 - par)

                sweep(dve, body)
                meanwhile()
                finish(NSEQ - 1, 1)

            dve.wait_ge(h0_ready, NSEQ)
            def experts_of(i, par):
                if not known(i) or i >= 2:
                    dve.wait_ge(f0.l1_ps, i - 1)
                    dve.wait_ge(f0.h1_ready, i - 1)
                    dve.wait_ge(f0.h2_ready, i - 1)
                dve.wait_ge(routed_in[par], i * (8 * NG) + (16 - 8 * par) * NG)
                for g in range(NG):
                    ins = v.tensor_tensor(WC[:, par, g, :], WR[:, par, g, :], WS[:, :], ALU.add)
                ins.then_inc(f0.wc_ready, 1)

            attention(a0, f0, count[0], 0, lambda: experts_of(0, 0))

            base = count[0] + 2 * NSEQ

            def group(ap, g):
                return ap.rearrange("k (t g p) -> k g t p", t=NT, g=NG)[:, g, :, :]

            def layer1(i, par):
                dve.wait_ge(f0.l1_ps, i + 1)
                for g in range(NG):
                    ins = v.tensor_scalar(group(F2[:, par, :], g), group(bank[3][:, :], g),
                                          WC[:, par, g, WROW + HID:WROW + HID + 1], 0.0, ALU.add, ALU.max)
                ins.then_inc(f0.h2_ready, 1)

            def add_back(s, i):
                dve.wait_ge(s.back_ps, i + 1)
                v.tensor_tensor(hb(i), hb(i), bank[7][:, :].rearrange("p (t d) -> p t d", t=NT)[:, :, 0:D],
                                ALU.add).then_inc(s.h_done, 1)

            def ffn0(i, par):
                if not known(i) or i >= 3:
                    add_back(f0, i - 3)
                sum_on(f0, a1, i + 5, 1 - par)
                if not known(i) or i >= 1:
                    layer1(i - 1, 1 - par)
                squares_on(f0, a1, i + 4, par)
                if has(i + 1):
                    experts_of(i + 1, 1 - par)

            sweep(dve, ffn0)
            add_back(f0, NSEQ - 3)
            layer1(NSEQ - 1, 1)
            add_back(f0, NSEQ - 2)
            add_back(f0, NSEQ - 1)

            GATE = 2 * NT + 4
            v.memset(g16[:, :, :], NONE).then_inc(gate_chain, 1)
            dve.wait_ge(gate_chain, 1)

            def gate_sum(i):
                c = 1 + i * GATE
                dve.wait_ge(f1.g_ps, i + 1)
                o = bank[1][:, 0:NT * 2 * NEXP1].rearrange("p (t a e) -> p t a e", t=NT, a=2)
                v.tensor_tensor(gs[:, :, :], o[:, :, 0, :],
                                w("bg").unsqueeze(1).to_broadcast([P, NT, NEXP1]), ALU.add).then_inc(gate_chain, 1)
                dve.wait_ge(gate_chain, c + 1)
                v.tensor_tensor(g16[:, :, 0:NEXP1], o[:, :, 1, :], gs[:, :, :], ALU.add).then_inc(gate_chain, 1)

            def gate_sort(i, meanwhile):
                dve.wait_ge(gate_chain, 1 + i * GATE + 2)
                meanwhile()
                for t in range(NT):
                    v.max(top[:, t, :], g16[:, t, 0:NEXP1]).then_inc(gate_chain, 1)

            def gate_choose(i, meanwhile):
                c = 1 + i * GATE
                dve.wait_ge(gate_chain, c + 2 + NT)
                v.memset(top[:, :, TOPK:], NONE).then_inc(gate_chain, 1)
                dve.wait_ge(gate_chain, c + 3 + NT)
                meanwhile()
                for t in range(NT):
                    v.match_replace(took[:, t, :], top[:, t, :], g16[:, t, :], TAKEN).then_inc(gate_chain, 1)

            def gate_masks(i):
                c = 1 + i * GATE
                dve.wait_ge(gate_chain, c + 3 + 2 * NT)
                if not known(i) or i >= 1:
                    dve.wait_ge(f1.mt_ps, i)
                v.tensor_scalar(MK[:, :, D:D + NEXP1], took[:, :, 0:NEXP1], TAKEN / 2, -1.0,
                                ALU.is_lt, ALU.mult).then_inc(gate_chain, 1)
                v.tensor_scalar(MK[:, :, D + NEXP1:D + 2 * NEXP1], took[:, :, 0:NEXP1], TAKEN / 2, None,
                                ALU.is_gt).then_inc(f1.mk_ready, 1)

            def copy_xh(i, par):
                dve.wait_ge(f1.x2_ready, i + 1)
                if not known(i) or i >= 2:
                    dve.wait_ge(f1.b2_ps, i - 1)
                    dve.wait_ge(f1.u_ps, i * NEXP1 - NEXP1)
                else:
                    dve.wait_ge(a1.st_ps, (NSEQ - 1 + i) * NT)
                v.tensor_copy(K2[0:D, par, :], f32(X2[0:D, par, :])).then_inc(f1.xh_ready, 1)

            def first_gate():
                copy_xh(0, 0)
                gate_sum(0)
                gate_sort(0, lambda: None)
                gate_choose(0, lambda: None)
                gate_masks(0)

            attention(a1, f1, base, 1, first_gate)

            def high(i, e):
                dve.wait_ge(f1.gelu_ready, i * NEXP1 + (e + 1))
                if not known(i) or i >= 1:
                    dve.wait_ge(f1.down_ps, i * NEXP1 + (e - 7))
                v.tensor_copy(GH[:, e, :], G[:, e, :]).then_inc(f1.high_ready, 1)

            def low(i, e):
                dve.wait_ge(f1.high_ready, i * NEXP1 + (e + 1))
                v.tensor_tensor(GL[:, e, :], G[:, e, :], f32(GH[:, e, :]), ALU.subtract).then_inc(f1.low_dve, 1)

            def add_halves(i):
                dve.wait_ge(f1.back_ps, i + 1)
                o = bank[7][:, :].rearrange("p (t d) -> p t d", t=NT)
                v.tensor_tensor(hb(i), hb(i), o[:, :, 0:D], ALU.add).then_inc(f1.h_half, 1)
                dve.wait_ge(f1.h_half, i + 1)
                v.tensor_tensor(hb(i), hb(i), o[:, :, D:2 * D], ALU.add).then_inc(f1.h_done, 1)


            def ffn1(i, par):
                if not known(i) or i >= 2:
                    add_halves(i - 2)
                high(i, 0)
                if has(i + 1):
                    gate_sum(i + 1)
                low(i, 0)
                if has(i + 1):
                    gate_sort(i + 1, lambda: high(i, 1))
                else:
                    high(i, 1)
                if has(i + 1):
                    gate_choose(i + 1, lambda: high(i, 2))
                else:
                    high(i, 2)
                low(i, 2)
                if has(i + 1):
                    gate_masks(i + 1)
                high(i, 3)
                if has(i + 1):
                    copy_xh(i + 1, 1 - par)
                high(i, 4)
                squares_on(f1, None, i + 4, par)
                sum_on(f1, None, i + 5, 1 - par)
                low(i, 4)
                high(i, 5)
                high(i, 6)
                low(i, 6)
                high(i, 7)

            sweep(dve, ffn1)
            add_halves(NSEQ - 2)
            add_halves(NSEQ - 1)

        @block.tensor
        def _(pe):
            mm = nc.tensor.matmul

            pe.wait_ge(parts_ready, PARTS)
            pe.wait_ge(consts_set, CONSTS)
            def embed(i, slot):
                pe.wait_ge(oh_ready, i + 1)
                pe.wait_ge(op_ready, i + 1)
                if not known(i) or i >= 2:
                    pe.wait_ge(h0_ready, i - 1)
                for t in range(NT):
                    o = bank[slot % 2][:, t * D:(t + 1) * D]
                    cols = slice(t * P, (t + 1) * P)
                    for k in range(PARTS):
                        mm(o, OH[:, slot, cols], T3[:, 0, k, :], start=(k == 0), stop=False)
                    last = mm(o, OP[:, slot, cols], TP[:, :], start=False, stop=True)
                last.then_inc(emb_ready, 1)

            for i in range(EARLY):
                embed(i, i % HOTS)
            pe.wait_ge(pack_in, 16 * PIECES)
            mm(bank[5][:, 0:P], w("wq0", D), w("wk0", D), start=True, stop=True)
            mm(bank[6][:, 0:D], w("wv", D), w("wo1", D), start=True, stop=True)
            mm(bank[7][:, 0:D], w("bvc", D + 1), w("wo1", D + 1), start=True, stop=True).then_inc(prod_ready, 1)
            with pe.Fori(EARLY // HOTS, NSEQ // HOTS) as four:
                for k in range(HOTS):
                    embed(four * HOTS + k, k)

            def turn(s, i, par):
                pe.wait_ge(s.xs_ready, i + 1)
                for t in range(NT):
                    last = nc.tensor.transpose(bank[0][:, t * P:(t + 1) * P], f32(XS[:, par, t, :]), w("ident"))
                last.then_inc(s.xt_ready, 1)

            def turn_on(s, after, i, par):
                if has(i):
                    turn(s, i, par)
                    return
                if i > NSEQ:
                    pe.wait_ge(after.x2_ready, i - NSEQ)
                else:
                    pe.wait_ge(s.x2_ready, NSEQ)
                turn(after, i - NSEQ, par)

            def turn_back(s, before, i, par):
                pe.wait_ge(s.ot_ready, i + 1)
                if not known(i) or i >= 1:
                    pe.wait_ge(s.h_done, i)
                elif before is not None:
                    pe.wait_ge(before.h_done, NSEQ)
                for t in range(NT):
                    last = nc.tensor.transpose(bank[7][:, t * P:(t + 1) * P], OT[:, par, t * P:(t + 1) * P],
                                               w("ident"))
                last.then_inc(s.back_ps, 1)

            def attention(s, before, after, layer, meanwhile, rest_before=None):
                keys = X2 if layer == 0 else KS

                def project(i, par):
                    pe.wait_ge(s.x2_ready, i + 1)
                    if not known(i) or i >= 1:
                        pe.wait_ge(s.ql_ready, i)
                    hi, lo = (AH[:, :], AL[:, :]) if layer == 0 else (wh("wq1"), wl("wq1"))
                    mm(bank[1][:, :], hi, X2[:, par, :], start=True, stop=False)
                    mm(bank[1][:, :], lo, X2[:, par, :], start=False, stop=True).then_inc(s.q_ps, 1)
                    if layer == 0:
                        return
                    if not known(i) or i >= 1:
                        pe.wait_ge(s.max_ready, i * NT)
                    mm(bank[3][:, :], wh("wk1"), X2[:, par, :], start=True, stop=False)
                    mm(bank[3][:, :], wl("wk1"), X2[:, par, :], start=False, stop=True).then_inc(s.k_ps, 1)
                    for t in range(NT):
                        last = mm(bank[2][:, t * P:(t + 1) * P], X2[:, par, t * P:(t + 1) * P], VHL[:, :],
                                  start=True, stop=True)
                    last.then_inc(s.v_ps, 1)

                def scores_for_max(i, par, t):
                    if t == 0:
                        pe.wait_ge(s.qh_ready, i + 1)
                        if layer == 1:
                            pe.wait_ge(s.kl_ready, i + 1)
                            pe.wait_ge(s.v_ready, i + 1)
                    if t >= 2:
                        pe.wait_ge(s.max_ready, i * NT + (t - 1))
                    elif not known(i) or i >= 1:
                        pe.wait_ge(s.max_ready, i * NT + (t - 1))
                    mm(bank[2 + t % 2][:, :], QH[:, par, t * P:(t + 1) * P], keys[:, par, :],
                       start=True, stop=True).then_inc(s.s_ps, 1)

                def spread_max(i, par):
                    pe.wait_ge(s.max_ready, i * NT + NT)
                    if before is not None and known(i) and i == 0:
                        pe.wait_ge(before.h_done, NSEQ)
                    if not known(i) or i >= 1:
                        pe.wait_ge(s.m_ready, i)
                    if not known(i) or i >= 2:
                        pe.wait_ge(s.h_done, i - 1)
                    for t in range(NT):
                        last = mm(bank[7][:, t * P:(t + 1) * P], nmax[:, par, t:t + 1].to_broadcast([P, P]),
                                  IR[:, :], start=True, stop=True)
                    last.then_inc(s.m_ps, 1)

                def scores(i, par, kt):
                    if kt == 0:
                        pe.wait_ge(s.m_ready, i + 1)
                        pe.wait_ge(s.ql_ready, i + 1)
                        pe.wait_ge(s.k2_ready, i + 1)
                    if kt >= 2 or not known(i) or i >= 1:
                        pe.wait_ge(s.e_ready, i * NT + (kt - 1))
                    cols = slice(kt * P, (kt + 1) * P)
                    o = bank[4 + kt % 2][:, :]
                    mm(o, keys[:, par, cols], QH[:, par, :], start=True, stop=False)
                    mm(o, K2[0:D + 1, par, cols], Q2[0:D + 1, par, :], start=False, stop=True).then_inc(s.st_ps, 1)

                def values(i, par, kt):
                    pe.wait_ge(s.e_ready, i * NT + (kt + 1))
                    if kt == 0:
                        pe.wait_ge(s.v_ready, i + 1)
                        if not known(i) or i >= 1:
                            pe.wait_ge(s.ot_ready, i)
                    last = mm(bank[6][0:D + 1, :], V1[:, par, kt, :], PT[:, par, kt, :],
                              start=(kt == 0), stop=(kt == NT - 1))
                    if kt == NT - 1:
                        last.then_inc(s.o_ps, 1)

                if before is None:
                    turn(s, 0, 0)
                else:
                    pe.wait_ge(before.h0_ready, NSEQ)
                    pe.wait_ge(before.h1_ready, NSEQ)
                    pe.wait_ge(before.h2_ready, NSEQ)
                project(0, 0)
                if before is None:
                    turn(s, 1, 1)
                else:
                    rest_before()
                for t in range(NT):
                    scores_for_max(0, 0, t)

                def body(i, par):
                    spread_max(i, par)
                    if has(i + 1):
                        project(i + 1, 1 - par)
                    turn_on(s, after, i + 2, par)
                    scores(i, par, 0)
                    scores(i, par, 1)
                    if not known(i) or i >= 1:
                        turn_back(s, before, i - 1, 1 - par)
                    scores(i, par, 2)
                    scores(i, par, 3)
                    if has(i + 1):
                        scores_for_max(i + 1, 1 - par, 0)
                        scores_for_max(i + 1, 1 - par, 1)
                    if not has(i + 1):
                        pe.wait_ge(s.ql_ready, NSEQ)
                        meanwhile()
                    values(i, par, 0)
                    values(i, par, 1)
                    if has(i + 1):
                        scores_for_max(i + 1, 1 - par, 2)
                        scores_for_max(i + 1, 1 - par, 3)
                    values(i, par, 2)
                    values(i, par, 3)

                sweep(pe, body)
                turn_back(s, before, NSEQ - 1, 1)

            pe.wait_ge(prod_read, 1)
            pe.wait_ge(high_set, HIGHS + 1)
            pe.wait_ge(low_set, LOWS)
            pe.wait_ge(h0_ready, NSEQ)
            def group(ap, g):
                return ap.rearrange("k (t g p) -> k g t p", t=NT, g=NG)[:, g, :, :]

            def enter0(i, par):
                pe.wait_ge(f0.x2_ready, i + 1)
                if not known(i) or i >= 1:
                    pe.wait_ge(f0.h0_ready, i)
                mm(bank[1][:, :], wh("wi"), X2[:, par, :], start=True, stop=False)
                mm(bank[1][:, :], wl("wi"), X2[:, par, :], start=False, stop=True).then_inc(f0.wi_ps, 1)

            def routed(i, par, l):
                src, dst, done = (F0, bank[2], f0.l0_ps) if l == 0 else (F1, bank[3], f0.l1_ps)
                if l == 0:
                    pe.wait_ge(f0.wc_ready, i + 1)
                    pe.wait_ge(f0.h0_ready, i + 1)
                    if not known(i) or i >= 1:
                        pe.wait_ge(f0.h1_ready, i)
                else:
                    pe.wait_ge(f0.h1_ready, i + 1)
                    if not known(i) or i >= 1:
                        pe.wait_ge(f0.h2_ready, i)
                for g in range(NG):
                    last = mm(group(dst[:, :], g), WC[:, par, g, l * WROW:l * WROW + HID],
                              group(src[:, par, :], g), start=True, stop=True)
                last.then_inc(done, 1)

            def leave0(i, par):
                pe.wait_ge(f0.h2_ready, i + 1)
                if not known(i) or i >= 1:
                    pe.wait_ge(f0.ot_ready, i)
                mm(bank[4][0:D, :], w("wo0"), F2[:, par, :], start=True, stop=True).then_inc(f0.o_ps, 1)

            attention(a0, None, f0, 0, lambda: enter0(0, 0))
            pe.wait_ge(a0.max_ready, NSEQ * NT)
            pe.wait_ge(a0.e_ready, NSEQ * NT)

            def ffn0(i, par):
                if has(i + 2):
                    pe.wait_ge(f0.x2_ready, i + 2)
                turn_on(f0, a1, i + 2, par)
                if has(i + 1):
                    enter0(i + 1, 1 - par)
                if not known(i) or i >= 2:
                    leave0(i - 2, par)
                if not known(i) or i >= 3:
                    turn_back(f0, a0, i - 3, 1 - par)
                if not known(i) or i >= 1:
                    routed(i - 1, 1 - par, 1)
                routed(i, par, 0)

            sweep(pe, ffn0)
            turn_back(f0, a0, NSEQ - 3, 1)
            leave0(NSEQ - 2, 0)
            routed(NSEQ - 1, 1, 1)
            turn_back(f0, a0, NSEQ - 2, 0)

            def last_turns():
                leave0(NSEQ - 1, 1)
                turn_back(f0, a0, NSEQ - 1, 1)
                pe.wait_ge(f0.ot_ready, NSEQ)

            def gate_scores(i, par):
                pe.wait_ge(f1.x2_ready, i + 1)
                if not known(i) or i >= 1:
                    pe.wait_ge(f1.mk_ready, i)
                for t in range(NT):
                    last = mm(bank[1][:, t * 2 * NEXP1:(t + 1) * 2 * NEXP1], X2[:, par, t * P:(t + 1) * P],
                              GHL[:, :], start=True, stop=True)
                last.then_inc(f1.g_ps, 1)

            def turn_masks(i, par):
                pe.wait_ge(f1.mk_ready, i + 1)
                if not known(i) or i >= 1:
                    pe.wait_ge(f1.m2_ready, i)
                for t in range(NT):
                    last = mm(bank[2][:, t * P:(t + 1) * P], MK[:, t, :], IB[:, :], start=True, stop=True)
                last.then_inc(f1.mt_ps, 1)

            def up(i, par, e):
                if e == 0:
                    pe.wait_ge(f1.xh_ready, i + 1)
                    pe.wait_ge(f1.m2_ready, i + 1)
                if e >= 2:
                    pe.wait_ge(f1.gelu_ready, i * NEXP1 + (e - 1))
                elif not known(i) or i >= 1:
                    pe.wait_ge(f1.gelu_ready, i * NEXP1 + (e - 1))
                a = at["w1"][0] + e * HID
                o = bank[3 + e % 2][:, :]
                mm(o, WH[:, a:a + HID], X2[:, par, :], start=True, stop=False)
                mm(o, WL[0:D + 2 * NEXP1, a:a + HID], K2[0:D + 2 * NEXP1, par, :], start=False, stop=True)\
                    .then_inc(f1.u_ps, 1)

            def down_bias(i, par):
                if not known(i) or i >= 2:
                    pe.wait_ge(f1.ot_ready, i - 1)
                rows = D + 2 * NEXP1
                mm(bank[5 + par][:, :], B2[0:rows, :], K2[0:rows, par, :], start=True, stop=False)\
                    .then_inc(f1.b2_ps, 1)

            def down(i, par, e):
                split = f1.low_dve if e % 2 == 0 else f1.low_pool
                pe.wait_ge(split, i * 4 + (e // 2 + 1))
                o = bank[5 + par][:, :]
                mm(o, W2[:, e, :], GH[:, e, :], start=False, stop=False)
                last = mm(o, W2[:, e, :], GL[:, e, :], start=False, stop=(e == NEXP1 - 1))
                last.then_inc(f1.down_ps, 1)

            attention(a1, f0, f1, 1, lambda: gate_scores(0, 0), last_turns)
            pe.wait_ge(a1.max_ready, NSEQ * NT)
            pe.wait_ge(a1.e_ready, NSEQ * NT)
            turn_masks(0, 0)
            pe.wait_ge(a1.ot_ready, NSEQ)

            def ffn1(i, par):
                for e in range(NEXP1):
                    up(i, par, e)
                    if e < LAG:
                        if not known(i) or i >= 1:
                            down(i - 1, 1 - par, e + NEXP1 - LAG)
                    else:
                        if e == LAG:
                            down_bias(i, par)
                        down(i, par, e - LAG)
                    if e == 0 and has(i + 1):
                        gate_scores(i + 1, 1 - par)
                    if e == 5 and has(i + 1):
                        turn_masks(i + 1, 1 - par)
                    if e == 7 and (not known(i) or i >= 1):
                        turn_back(f1, a1, i - 1, 1 - par)
                if has(i + 2):
                    pe.wait_ge(f1.x2_ready, i + 2)
                    turn(f1, i + 2, par)

            sweep(pe, ffn1)
            for e in range(NEXP1 - LAG, NEXP1):
                down(NSEQ - 1, 1, e)
            turn_back(f1, a1, NSEQ - 1, 1)


def kernel(**inputs):
    import concourse.bacc as bacc
    from concourse.bass_utils import run_bass_kernel_spmd

    x = {k: np.asarray(v) for k, v in inputs.items()}
    at, width = columns()
    pack = np.zeros((P, width), np.float32)

    def put(name, value, row=0):
        value = np.asarray(value)
        if value.ndim == 1:
            value = value[:, None]
        a = at[name][0]
        pack[row:row + value.shape[0], a:a + value.shape[1]] = value

    def twice(m):
        return np.concatenate([m, m], 0)

    def wide(m):
        return np.concatenate([m, m], 1)

    put("wq0", wide(x["L0_attn_Wq"]))
    put("wk0", wide(x["L0_attn_Wk"]))
    put("wq1", twice(wide(x["L1_attn_Wq"].T)))
    put("wk1", twice(wide(x["L1_attn_Wk"].T)))
    put("bq", twice(x["L1_attn_bq"][:, None]))
    put("bk", twice(x["L1_attn_bk"][:, None]))
    put("wv", wide(x["L1_attn_Wv"]))
    put("wo1", x["L1_attn_Wo"].T)
    put("wo1", x["L1_attn_bo"][None, :], D)
    put("bvc", np.broadcast_to(x["L1_attn_bv"][:, None], (D, P)))
    put("bvc", np.ones((1, P), np.float32), D)
    put("wi", twice(x["L0_ffn_Wi"].T))
    put("bi", x["L0_ffn_bi"])
    put("wo0", x["L0_ffn_Wo"].T)
    put("bo0", x["L0_ffn_bo"])
    put("w1", twice(x["L1_ffn_W1"].transpose(1, 0, 2).reshape(D, NEXP1 * HID)))
    put("b1", x["L1_ffn_b1"].T)
    put("w2", x["L1_ffn_W2"].transpose(1, 0, 2).reshape(HID, NEXP1 * D))
    put("b2", x["L1_ffn_b2"], D + NEXP1)
    put("wg", twice(x["L1_ffn_Wg"]))
    put("bg", np.broadcast_to(x["L1_ffn_bg"][None, :], (P, NEXP1)))
    put("tok", x["L0_tok_token_W"])
    put("pe", np.concatenate([x["L0_tok_pe"][:NSEQ]] * PARTS, 0))
    ws = np.zeros((P, NLAY0, WROW), np.float32)
    ws[:, :, :HID] = x["L0_ffn_Ws"][:, 0].transpose(2, 0, 1)
    ws[:, :, HID] = x["L0_ffn_bs"][:, 0].T
    put("ws", ws.reshape(P, NLAY0 * WROW))
    experts = np.zeros((NEXP0, P, NLAY0, WROW), np.float32)
    experts[:, :, :, :HID] = x["L0_ffn_Wr"].transpose(1, 3, 0, 2)
    experts[:, :, :, HID] = x["L0_ffn_br"].transpose(1, 2, 0)
    put("ident", np.eye(P, dtype=np.float32))
    put("iota", np.arange(P, dtype=np.float32))
    put("row", np.tile(np.arange(NSEQ, dtype=np.float32), PARTS))

    nc = bacc.Bacc("TRN2", target_bir_lowering=False, num_devices=1)
    arrays = {
        "tokens": np.ascontiguousarray(x["x"]),
        "route": np.ascontiguousarray(x["L0_ffn_route_id"].reshape(1, -1)),
        "pack": pack,
        "experts": experts.reshape(NEXP0, P, NLAY0 * WROW),
    }
    args = [nc.dram_tensor(n, a.shape, mybir.dt.from_np(a.dtype), kind="ExternalInput").ap()
            for n, a in arrays.items()]
    out = nc.dram_tensor("out", (NSEQ, SEQ, D), F32, kind="ExternalOutput").ap()
    ids = nc.dram_tensor("ids", (NSEQ, SEQ), BF16, kind="Internal").ap()
    pos = nc.dram_tensor("pos", (NSEQ, SEQ), BF16, kind="Internal").ap()
    tower_kernel(nc, *args, out, ids, pos)
    result = run_bass_kernel_spmd(nc, [arrays], core_ids=[0])
    return result.results[0]["out"]
```
